# Optimizing a Trainium2 kernel written in Bass

```python
import numpy as np
import jax
import jax.numpy as jnp

def _softmax(x, axis=-1):
    return jax.nn.softmax(x, axis=axis)

def _gelu(x):
    return jax.nn.gelu(x, approximate=True)

def _silu(x):
    return jax.nn.silu(x)

def _sigmoid(x):
    return jax.nn.sigmoid(x)

def _layernorm(x, axis=-1, eps=1e-05):
    m = jnp.mean(x, axis=axis, keepdims=True)
    v = jnp.var(x, axis=axis, keepdims=True)
    return (x - m) / jnp.sqrt(v + eps)

def _scatter_add(tgt, idx, src, axis=0):
    return tgt.at[idx].add(src)

def _segment_sum(src, seg, n):
    return jax.ops.segment_sum(src, seg, n)
kernel_name = 'mk_seq_preln_d1_jaxref_r8_f2696e'

def setup_inputs(seed: int=0):
    np.random.seed(seed)
    _w = jnp.asarray

    def _L0_attn_setup():
        import jax, jax.numpy as jnp
        import numpy as np
        NUM_HEADS = 16
        HIDDEN = 128
        HEAD = HIDDEN // NUM_HEADS
        key = jax.random.key(seed)
        k1, k2 = jax.random.split(key)
        embeddings = jax.random.normal(k1, (4, 256, HIDDEN), dtype=jnp.float32)
        w_qkv = jax.random.normal(k2, (HIDDEN, 3 * HIDDEN), dtype=jnp.float32) * (1.0 / np.sqrt(HIDDEN))
        return {'embeddings': embeddings, 'w_qkv': w_qkv}
    _L0_attn_in = _L0_attn_setup()

    def _L0_ffn_setup():
        import jax, jax.numpy as jnp
        import numpy as np
        EPS = 1e-09
        key = jax.random.key(seed)
        k1, k2, k3, k4 = jax.random.split(key, 4)
        B, T, H, D, E = (2, 256, 128, 128, 8)
        x = jax.random.normal(k1, (B, T, H), dtype=jnp.float32)
        gate_w = jax.random.normal(k2, (E, H), dtype=jnp.float32) * 0.02
        gate_up_proj = jax.random.normal(k3, (E, H, 2 * D), dtype=jnp.float32) * 0.02
        down_proj = jax.random.normal(k4, (E, D, H), dtype=jnp.float32) * 0.02
        return {'x': x, 'gate_w': gate_w, 'gate_up_proj': gate_up_proj, 'down_proj': down_proj}
    _L0_ffn_in = _L0_ffn_setup()
    _d = {'L0_attn_embeddings': _L0_attn_in['embeddings'], 'L0_attn_w_qkv': _L0_attn_in['w_qkv'], 'L0_ffn_gate_w': _L0_ffn_in['gate_w'], 'L0_ffn_gate_up_proj': _L0_ffn_in['gate_up_proj'], 'L0_ffn_down_proj': _L0_ffn_in['down_proj']}
    _x0 = _d['L0_attn_embeddings']
    _d['L0_attn_embeddings'] = jax.random.normal(jax.random.fold_in(jax.random.key(seed), 1), (16, 512, 128), dtype=_x0.dtype)
    del _x0
    return _d

def reference(L0_attn_embeddings, L0_attn_w_qkv, L0_ffn_gate_w, L0_ffn_gate_up_proj, L0_ffn_down_proj):

    def _L0_attn_ref(embeddings, w_qkv):
        import jax, jax.numpy as jnp
        import numpy as np
        NUM_HEADS = 16
        HIDDEN = 128
        HEAD = HIDDEN // NUM_HEADS
        b, s, h = embeddings.shape
        result = embeddings @ w_qkv
        result = result.reshape(b, s, 3, NUM_HEADS, HEAD)
        q = jnp.transpose(result[:, :, 0], (0, 2, 1, 3))
        k = jnp.transpose(result[:, :, 1], (0, 2, 1, 3))
        v = jnp.transpose(result[:, :, 2], (0, 2, 1, 3))
        scores = jnp.einsum('bnqd,bnkd->bnqk', q, k) / jnp.sqrt(jnp.float32(h))
        probs = jax.nn.softmax(scores, axis=-1)
        ctx = jnp.einsum('bnqk,bnkd->bnqd', probs, v)
        out = jnp.transpose(ctx, (0, 2, 1, 3)).reshape(b, s, h)
        return out

    def _L0_ffn_ref(x, gate_w, gate_up_proj, down_proj):
        import jax, jax.numpy as jnp
        import numpy as np
        EPS = 1e-09
        B, T, H = x.shape
        E = gate_w.shape[0]
        top_k = 2
        hidden = x.reshape(-1, H)
        router_logits = hidden @ gate_w.T
        routing_weights = jax.nn.softmax(router_logits.astype(jnp.float32), axis=-1)
        topk_weights, topk_indices = jax.lax.top_k(routing_weights, top_k)
        topk_weights = topk_weights / (jnp.sum(topk_weights, axis=-1, keepdims=True) + EPS)
        N = hidden.shape[0]
        routed = jnp.zeros((N, E), dtype=router_logits.dtype)
        rows = jnp.arange(N)[:, None]
        routed = routed.at[rows, topk_indices].set(topk_weights.astype(router_logits.dtype))
        routed = routed / (jnp.sum(routed, axis=-1, keepdims=True) + EPS)
        routed = routed.astype(hidden.dtype)
        gate_up = jnp.einsum('th,ehq->teq', hidden, gate_up_proj)
        gate, up = jnp.split(gate_up, 2, axis=-1)
        expert_outputs = jnp.einsum('teq,eqh->teh', jax.nn.silu(gate) * up, down_proj)
        out = jnp.sum(expert_outputs * routed[:, :, None], axis=1)
        return out.reshape(B, T, H)
    x = L0_attn_embeddings
    x = x + _L0_attn_ref(_layernorm(x, axis=-1), L0_attn_w_qkv)
    x = x + _L0_ffn_ref(_layernorm(x, axis=-1), L0_ffn_gate_w, L0_ffn_gate_up_proj, L0_ffn_down_proj)
    return x

_drawn_inputs = setup_inputs


def setup_inputs(seed=0):
    import zlib

    import numpy as np

    out = dict(_drawn_inputs(seed))
    spreads = {}
    factors = {'L0_ffn_gate_w': 8.0, 'L0_ffn_gate_up_proj': 8.0, 'L0_ffn_down_proj': 8.0}
    for name, (base, spread) in spreads.items():
        noise = np.random.default_rng([zlib.crc32(name.encode()), seed]).standard_normal(out[name].shape)
        drawn = base * np.exp(spread * noise) if base else spread * noise
        out[name] = jnp.asarray(drawn.astype(out[name].dtype))
    for name, factor in factors.items():
        out[name] = (out[name] * factor).astype(out[name].dtype)
    return out
```

```python
import concourse.bass as bass
from concourse import mybir
from contextlib import ExitStack

FP32 = mybir.dt.float32
BF16 = mybir.dt.bfloat16
FP32R = mybir.dt.float32r
ALU = mybir.AluOpType
ACT = mybir.ActivationFunctionType
AX = mybir.AxisListType


class Step:

    def __init__(self, number, passes, unroll, least, most, batches):
        self.number, self.passes, self.unroll = number, passes, unroll
        self.least, self.most, self.batches = least, most, batches
        self.slot = least % unroll

    def buffer(self, ahead):
        return (self.least + ahead) % self.unroll

    def loads(self, ahead):
        return self.passes * 16 + 16 * ((self.least + ahead) // self.unroll + 1)

    def has(self, ahead):
        first, last = self.least + ahead, self.most + ahead
        assert (0 <= first and last < self.batches) or first == last or last < 0 or first >= self.batches
        return 0 <= first and last < self.batches

    def count(self, per_batch, ahead, k):
        least = per_batch * (self.least + ahead) + k
        if self.least == self.most:
            return max(least, 0)
        assert least > 0
        return self.number * per_batch + (per_batch * ahead + k)


def walk(engine, before, unroll, loops, after, batches):
    for s in before:
        yield Step(s, 0, unroll, s, s, batches)
    first = before[-1] + 1
    with engine.Fori(0, loops) as i:
        for k in range(first, first + unroll):
            yield Step(i * unroll + k, i, unroll, k, k + (loops - 1) * unroll, batches)
    for s in after:
        yield Step(s, 0, unroll, s, s, batches)


def attention_moe_kernel(
    nc: bass.Bass,
    x: bass.AP,
    w_qkv: bass.AP,
    gate_w: bass.AP,
    gate_up_proj: bass.AP,
    down_proj: bass.AP,
    identity: bass.AP,
    out: bass.AP,
):
    B, S, H = x.shape
    E = gate_w.shape[1]
    NH = 16
    D = H // NH
    NT = S // 128
    LN_EPS = 1e-5
    TOP_EPS = 1e-9
    SCALE = float(H) ** -0.5

    Q_PARTS = (0, 0, 0, 1, 1, 2)
    K_PARTS = (0, 1, 2, 0, 1, 0)
    PARTS = 3
    MAX_ROW = 96
    GH = 4
    NG = NH // GH
    UNITS = NG * NT
    HALF = NH // 2
    TILES = NH * NT
    BANKS = 3

    def bank_free(tile):
        if tile >= BANKS:
            return tile - BANKS + 1
        before = [n for n in range(TILES) if n % BANKS == tile]
        return before[-1] + 1 - TILES

    MAX_TILES = [5] * 12 + [4] + [0] * 3
    assert sum(MAX_TILES) == TILES
    AT_CTX, AT_XT, AT_Q, AT_K, AT_V, AT_MAX = 3, 4, 6, 8, 10, 14

    x_v = x.rearrange("b (t p) h -> b p t h", p=128)
    out_v = out.rearrange("b (t p) h -> b p t h", p=128)
    q_scratch = nc.dram_tensor("q_scratch", (2, PARTS, NH, D, S), BF16, kind="Internal").ap()
    k_scratch = nc.dram_tensor("k_scratch", (2, PARTS, NH, D, S), BF16, kind="Internal").ap()
    max_scratch = nc.dram_tensor("max_scratch", (2, PARTS, NH, S), BF16, kind="Internal").ap()
    route_scratch = nc.dram_tensor("route_scratch", (3, E, NT, 128), FP32, kind="Internal").ap()

    with ExitStack() as whole:
        def sem(name, stack=whole):
            return stack.enter_context(nc.semaphore(name))

        def sb(name, shape, dtype, stack=whole):
            return stack.enter_context(nc.sbuf_tensor(name, shape, dtype))

        def ps(name, shape, dtype, stack=whole):
            return stack.enter_context(nc.psum_tensor(name, shape, dtype))

        stood = sem("stood")
        x_all = sb("x_all", [128, B * S], FP32)
        ident = sb("ident", [128, 128], FP32)
        w_gu = sb("w_gu", [128, E, 2 * H], FP32)
        w_down = sb("w_down", [128, E, H], FP32)
        w_gate = sb("w_gate", [128, E], FP32)
        w_gu_hi = sb("w_gu_hi", [128, E, 2 * H], FP32R)
        w_gu_lo = sb("w_gu_lo", [128, E, 2 * H], FP32R)
        w_gate_hi = sb("w_gate_hi", [128, E], FP32R)
        w_gate_lo = sb("w_gate_lo", [128, E], FP32R)
        earlier = sb("earlier", [128, NT, E, E], FP32)

        ln_var = sb("ln_var", [128, NT], FP32)
        minus_half = sb("minus_half", [128, NT], FP32)

        with ExitStack() as one:
            w_sb = sb("w_sb", [128, 3 * H], FP32, one)
            ident_bf = sb("ident_bf", [128, 128], BF16, one)
            xin = sb("xin", [128, 2, NT, H], FP32, one)
            ln_stats = sb("ln_stats", [128, NT, nc.vector.BN_STATS_DIM], FP32, one)
            ln_mv = sb("ln_mv", [128, 2, NT, 2], FP32, one)
            ln_rstd = sb("ln_rstd", [128, 2, NT], FP32, one)
            xn = sb("xn", [128, NT, H], FP32, one)
            xnT = sb("xnT", [128, 2, S], FP32, one)
            q_split = sb("q_split", [128, PARTS, S], BF16, one)
            k_split = sb("k_split", [128, PARTS, S], BF16, one)
            q_rest = sb("q_rest", [128, S], FP32, one)
            k_rest = sb("k_rest", [128, S], FP32, one)
            q_rows = [sb(f"q_rows{i}", [128, NH, S], BF16, one) for i in range(2)]
            k_rows = [sb(f"k_rows{i}", [128, NH, S], BF16, one) for i in range(2)]
            v_ext = [sb(f"v_ext{i}", [128, NT, NH, 32], FP32, one) for i in range(2)]
            neg_max = sb("neg_max", [128, NT, NH], FP32, one)
            max_rest = sb("max_rest", [128, NT, NH], FP32, one)
            max_split = sb("max_split", [128, NT, PARTS, NH], BF16, one)
            maxT = sb("maxT", [PARTS * NH, S], BF16, one)
            probs = sb("probs", [128, 2, GH, S], FP32, one)
            ctxT = sb("ctxT", [128, S], FP32, one)
            inv_sum = sb("inv_sum", [128, NT, GH], FP32, one)
            ctx_out = sb("ctx_out", [128, 2, NT, H], FP32, one)

            score_ps = ps("score_ps", [128, BANKS, S], FP32, one)
            max_ps = ps("max_ps", [128, BANKS, S], FP32, one)
            pv_ps = ps("pv_ps", [128, S], FP32, one)
            misc_ps = ps("misc_ps", [128, 512], FP32, one)
            maxT_ps = misc_ps[0:PARTS * NH, 0:S // 2].bitcast(BF16)

            weights_in = sem("weights_in", one)
            moe_weights_in = sem("moe_weights_in", one)
            x_all_in = sem("x_all_in", one)
            w_hi_done = sem("w_hi_done", one)
            xin_in = [sem(f"xin_in{i}", one) for i in range(2)]
            rows_zeroed = sem("rows_zeroed", one)
            earlier_zeroed = sem("earlier_zeroed", one)
            rows_preset = sem("rows_preset", one)
            v_zeroed = sem("v_zeroed", one)
            v_preset = sem("v_preset", one)
            ident_done = sem("ident_done", one)
            stats_done = sem("stats_done", one)
            mv_done = sem("mv_done", one)
            var_done = sem("var_done", one)
            rstd_done = sem("rstd_done", one)
            xn_done = sem("xn_done", one)
            xT_ready = sem("xT_ready", one)
            xnT_done = sem("xnT_done", one)
            q_ready = sem("q_ready", one)
            k_ready = sem("k_ready", one)
            v_ready = sem("v_ready", one)
            q_hi_done = sem("q_hi_done", one)
            k_hi_done = sem("k_hi_done", one)
            q_rest_done = sem("q_rest_done", one)
            k_rest_done = sem("k_rest_done", one)
            q_mid_done = sem("q_mid_done", one)
            k_mid_done = sem("k_mid_done", one)
            q_lo_done = sem("q_lo_done", one)
            k_lo_done = sem("k_lo_done", one)
            q_written = sem("q_written", one)
            k_written = sem("k_written", one)
            rows_in = [sem(f"rows_in{i}", one) for i in range(2)]
            v_done = sem("v_done", one)
            max_scored = sem("max_scored", one)
            max_taken = sem("max_taken", one)
            max_hi_done = sem("max_hi_done", one)
            max_rest_done = sem("max_rest_done", one)
            max_mid_done = sem("max_mid_done", one)
            max_split_done = sem("max_split_done", one)
            maxT_ready = sem("maxT_ready", one)
            maxT_done = sem("maxT_done", one)
            max_written = sem("max_written", one)
            max_rows_in = sem("max_rows_in", one)
            scored = sem("scored", one)
            probs_done = sem("probs_done", one)
            pv_done = sem("pv_done", one)
            ctxT_done = sem("ctxT_done", one)
            ctx_ready = sem("ctx_ready", one)
            inv_done = sem("inv_done", one)
            ctx_done = sem("ctx_done", one)
            x1_done = sem("x1_done", one)

            block = one.enter_context(nc.Block())

            def steps(engine):
                return walk(engine, (-2, -1, 0), 2, (B - 4) // 2, range(B - 3, B + 1), B)

            @block.sync
            def _(sp):
                def load_x(b):
                    sp.dma_start(xin[:, b % 2], x_v[b]).then_inc(xin_in[b % 2], 16)

                load_x(0)
                sp.dma_start(ident[:], identity).then_inc(weights_in, 16)
                sp.dma_start(w_sb[:], w_qkv).then_inc(weights_in, 16)
                for st in steps(sp):
                    p = st.slot
                    if st.has(3):
                        sp.wait_ge(xn_done, st.count(1, 1, 1))
                        sp.dma_start(xin[:, (p + 1) % 2], x_v[bass.ds(st.number + 3, 1)].rearrange(
                            "o p t h -> (o p) t h")).then_inc(xin_in[(p + 1) % 2], 16)
                    if st.least == st.most == -2:
                        sp.dma_start(x_all[:].rearrange("p (b t h) -> p b t h", b=B, t=NT),
                                     x_v.rearrange("b p t h -> p b t h")).then_inc(x_all_in, 16)
                        sp.dma_start(w_gu[:], gate_up_proj.rearrange("e h q -> h e q")).then_inc(moe_weights_in, 16)
                        sp.dma_start(w_down[:], down_proj.rearrange("e q h -> q e h")).then_inc(moe_weights_in, 16)
                        sp.dma_start(w_gate[:], gate_w).then_inc(moe_weights_in, 16)
                    if st.has(2):
                        for split, scratch, lo_done, written in (
                                (q_split, q_scratch, q_lo_done, q_written),
                                (k_split, k_scratch, k_lo_done, k_written)):
                            sp.wait_ge(lo_done, st.count(1, 2, 1))
                            for j in range(PARTS):
                                sp.dma_start(scratch[p, j].rearrange("h d s -> (h d) s"),
                                             split[:, j]).then_inc(written, 16)
                        sp.wait_ge(q_written, st.count(48, 2, 48))
                        sp.wait_ge(k_written, st.count(48, 2, 48))

                    def load_rows(half):
                        if st.has(0):
                            sp.wait_ge(scored, st.count(TILES, 0, TILES // 2 * (half + 1)))
                        sp.wait_ge(rows_in[half], st.count(192, 1, 192))
                        h = slice(half * HALF, (half + 1) * HALF)
                        for rows, scratch, parts in ((q_rows, q_scratch, Q_PARTS), (k_rows, k_scratch, K_PARTS)):
                            for n, j in enumerate(parts):
                                sp.dma_start(rows[p][n * D:(n + 1) * D, h, :],
                                             scratch[p, j, h].rearrange("h d s -> d h s")).then_inc(rows_in[half], 16)

                    if st.has(2):
                        if st.least == st.most == -2:
                            sp.wait_ge(rows_preset, 2)
                        load_rows(0)
                    if st.has(1):
                        sp.wait_ge(maxT_done, st.count(1, 1, 1))
                        o = (p + 1) % 2
                        sp.dma_start(max_scratch[o].rearrange("j h s -> (j h) s"), maxT[:]).then_inc(max_written, 16)
                        sp.wait_ge(max_written, st.count(16, 1, 16))
                        sp.dma_start(q_rows[o][MAX_ROW:MAX_ROW + PARTS, :, :], max_scratch[o]).then_inc(max_rows_in, 16)
                    if st.has(2):
                        load_rows(1)
                sp.wait_ge(moe_weights_in, 48)

            @block.gpsimd
            def _(pool):
                nc.gpsimd.memset(minus_half[:], -0.5).then_inc(x1_done, 1)
                nc.gpsimd.memset(k_rows[0][:], 0.0)
                nc.gpsimd.memset(k_rows[1][:], 0.0).then_inc(rows_zeroed, 1)
                nc.gpsimd.memset(earlier[:], 0.0).then_inc(earlier_zeroed, 1)
                pool.wait_ge(earlier_zeroed, 1)
                for e in range(1, E):
                    nc.gpsimd.memset(earlier[:, :, e, 0:e], 1.0)
                for st in steps(pool):
                    p = st.slot
                    if st.least == st.most == B - 3:
                        pool.wait_ge(moe_weights_in, 48)
                        nc.gpsimd.tensor_copy(w_gu_hi[:], w_gu[:])
                        nc.gpsimd.tensor_copy(w_gate_hi[:], w_gate[:]).then_inc(w_hi_done, 1)
                        pool.wait_ge(w_hi_done, 1)
                        nc.gpsimd.tensor_tensor(w_gu_lo[:], w_gu[:], w_gu_hi[:].bitcast(FP32), ALU.subtract)
                        nc.gpsimd.tensor_tensor(w_gate_lo[:], w_gate[:], w_gate_hi[:].bitcast(FP32), ALU.subtract)
                    if st.has(2):
                        pool.wait_ge(mv_done, st.count(1, 2, 1))
                        pool.sem_inc(stood, 1)
                        nc.gpsimd.tensor_scalar(ln_var[:], ln_mv[:, p, :, 1], LN_EPS, None, ALU.add).then_inc(var_done, 1)
                        pool.wait_ge(var_done, st.count(1, 2, 1))
                        pool.sem_inc(stood, 1)
                        nc.gpsimd.tensor_tensor(ln_rstd[:, p], ln_var[:], minus_half[:], ALU.pow).then_inc(rstd_done, 1)
                        pool.wait_ge(rstd_done, st.count(1, 2, 1))
                        pool.sem_inc(stood, 1)
                        pool.wait_ge(xT_ready, st.count(1, 1, 1))
                        pool.sem_inc(stood, 1)
                        for t in range(NT):
                            last = nc.gpsimd.tensor_scalar(xn[:, t], xin[:, p, t], ln_mv[:, p, t, 0:1],
                                                           ln_rstd[:, p, t:t + 1], ALU.subtract, ALU.mult)
                        last.then_inc(xn_done, 1)
                    if st.has(-1):
                        o = (p + 1) % 2
                        if st.least == 1 or st.least == st.most:
                            pool.wait_ge(x_all_in, 16)
                        pool.wait_ge(ctx_done, st.count(NG, -1, NG))
                        pool.sem_inc(stood, 1)
                        here = x_all[:, bass.ds((st.number - 1) * S, S)]
                        nc.gpsimd.tensor_tensor(here, here, ctx_out[:, o].rearrange("p t h -> p (t h)"),
                                                ALU.add).then_inc(x1_done, 1)
                    if st.has(2):
                        for rest, split, rest_done, mid_done, lo_done, written in (
                                (q_rest, q_split, q_rest_done, q_mid_done, q_lo_done, q_written),
                                (k_rest, k_split, k_rest_done, k_mid_done, k_lo_done, k_written)):
                            pool.wait_ge(rest_done, st.count(1, 2, 1))
                            pool.sem_inc(stood, 1)
                            pool.wait_ge(written, st.count(48, 1, 48))
                            pool.sem_inc(stood, 1)
                            nc.gpsimd.tensor_copy(split[:, 1], rest[:]).then_inc(mid_done, 1)
                            pool.wait_ge(mid_done, st.count(1, 2, 1))
                            pool.sem_inc(stood, 1)
                            nc.gpsimd.tensor_tensor(split[:, 2], rest[:], split[:, 1],
                                                    ALU.subtract).then_inc(lo_done, 1)

            @block.vector
            def _(dve):
                nc.vector.memset(q_rows[0][:], 0.0)
                nc.vector.memset(q_rows[1][:], 0.0).then_inc(rows_preset, 1)
                for v in v_ext:
                    last = nc.vector.memset(v[:], 0.0)
                last.then_inc(v_zeroed, 1)
                dve.wait_ge(rows_zeroed, 1)
                for rows in k_rows:
                    last = nc.vector.memset(rows[MAX_ROW:MAX_ROW + PARTS], 1.0)
                last.then_inc(rows_preset, 1)
                dve.wait_ge(weights_in, 32)
                nc.vector.tensor_copy(ident_bf[:], ident[:]).then_inc(ident_done, 1)
                dve.wait_ge(v_zeroed, 1)
                for v in v_ext:
                    last = nc.vector.memset(v[:, :, :, D:D + 1], 1.0)
                last.then_inc(v_preset, 1)
                for st in steps(dve):
                    p, o = st.slot, (st.slot + 1) % 2

                    def normal_stats():
                        dve.wait_ge(xin_in[st.buffer(2)], st.loads(2))
                        dve.wait_ge(mv_done, st.count(1, 1, 1))
                        for t in range(NT):
                            last = nc.vector.bn_stats(ln_stats[:, t], xin[:, p, t])
                        last.then_inc(stats_done, 1)
                        dve.wait_ge(xn_done, st.count(1, 0, 1))
                        dve.wait_ge(stats_done, st.count(1, 2, 1))
                        dve.sem_inc(stood, 1)
                        for t in range(NT):
                            last = nc.vector.bn_aggr(ln_mv[:, p, t], ln_stats[:, t])
                        last.then_inc(mv_done, 1)

                    def rest(split, rest_sb, hi_done, rest_done, lo_done):
                        dve.wait_ge(hi_done, st.count(1, 2, 1))
                        dve.wait_ge(lo_done, st.count(1, 1, 1))
                        nc.vector.tensor_tensor(rest_sb[:], misc_ps[:], split[:, 0],
                                                ALU.subtract).then_inc(rest_done, 1)

                    def normal_ctx(ahead, g):
                        out_p = (p + ahead) % 2
                        view = misc_ps[:].rearrange("p (t j i) -> p t j i", t=NT, j=GH)
                        dve.wait_ge(ctx_ready, st.count(NG, ahead, g + 1))
                        dve.wait_ge(ctx_done, st.count(NG, ahead, g))
                        nc.vector.reciprocal(inv_sum[:], view[:, :, :, D]).then_inc(inv_done, 1)
                        dve.wait_ge(inv_done, st.count(NG, ahead, g + 1))
                        if g == 0:
                            dve.wait_ge(x1_done, st.count(1, ahead - 2, 2))
                        nc.vector.tensor_tensor(
                            ctx_out[:, out_p].rearrange("p t (g j i) -> p t g j i", g=NG, j=GH)[:, :, g],
                            view[:, :, :, 0:D], inv_sum[:].unsqueeze(3).to_broadcast([128, NT, GH, D]),
                            ALU.mult).then_inc(ctx_done, 1)

                    if st.has(2):
                        normal_stats()
                    def between(u):
                        if st.has(2) and u == AT_Q:
                            rest(q_split, q_rest, q_hi_done, q_rest_done, q_lo_done)
                        if st.has(2) and u == AT_K:
                            rest(k_split, k_rest, k_hi_done, k_rest_done, k_lo_done)
                        if u == AT_CTX and st.has(-1):
                            normal_ctx(-1, NG - 1)
                        if u % NT == AT_CTX and u > AT_CTX and st.has(0):
                            normal_ctx(0, u // NT - 1)

                    tile = 0
                    for u in range(UNITS):
                        for n in range(GH + 1):
                            if n == 2:
                                between(u)
                            if n < MAX_TILES[u] and st.has(1):
                                dve.wait_ge(max_scored, st.count(TILES, 1, tile + 1))
                                if tile == 0:
                                    dve.wait_ge(max_split_done, st.count(1, 0, 1))
                                h, t = divmod(tile, NT)
                                nc.vector.reduce_max(neg_max[:, t, h:h + 1], max_ps[:, tile % BANKS], AX.X,
                                                     negate=True).then_inc(max_taken, 1)
                                tile += 1
                        if u == AT_MAX - 1 and st.has(1):
                            dve.wait_ge(max_taken, st.count(TILES, 1, TILES))
                            dve.wait_ge(maxT_ready, st.count(1, 0, 1))
                            nc.vector.tensor_copy(max_split[:, :, 0], neg_max[:]).then_inc(max_hi_done, 1)
                            dve.wait_ge(max_hi_done, st.count(1, 1, 1))
                            nc.vector.tensor_tensor(max_rest[:], neg_max[:], max_split[:, :, 0],
                                                    ALU.subtract).then_inc(max_rest_done, 1)
                            dve.wait_ge(max_rest_done, st.count(1, 1, 1))
                            nc.vector.tensor_copy(max_split[:, :, 1], max_rest[:]).then_inc(max_mid_done, 1)
                            dve.wait_ge(max_mid_done, st.count(1, 1, 1))
                            nc.vector.tensor_tensor(max_split[:, :, 2], max_rest[:], max_split[:, :, 1],
                                                    ALU.subtract).then_inc(max_split_done, 1)

            @block.scalar
            def _(act):
                for st in steps(act):
                    p, o = st.slot, (st.slot + 1) % 2

                    def take_context(ahead, g):
                        act.wait_ge(pv_done, st.count(UNITS, ahead, NT * (g + 1)))
                        act.wait_ge(ctx_ready, st.count(NG, ahead, g))
                        nc.scalar.copy(ctxT[:], pv_ps[:]).then_inc(ctxT_done, 1)

                    for u in range(UNITS):
                        if u == 1 and st.has(-1):
                            take_context(-1, NG - 1)
                        if u % NT == 1 and u > 1 and st.has(0):
                            take_context(0, u // NT - 1)
                        if u == AT_XT and st.has(2):
                            act.wait_ge(xT_ready, st.count(1, 2, 1))
                            act.wait_ge(v_ready, st.count(1, 0, 1))
                            nc.scalar.copy(xnT[:, p], misc_ps[:]).then_inc(xnT_done, 1)
                        if u == AT_Q and st.has(2):
                            act.wait_ge(q_ready, st.count(1, 2, 1))
                            act.wait_ge(q_written, st.count(48, 1, 48))
                            nc.scalar.copy(q_split[:, 0], misc_ps[:]).then_inc(q_hi_done, 1)
                        if u == AT_K and st.has(2):
                            act.wait_ge(k_ready, st.count(1, 2, 1))
                            act.wait_ge(k_written, st.count(48, 1, 48))
                            nc.scalar.copy(k_split[:, 0], misc_ps[:]).then_inc(k_hi_done, 1)
                        if u == AT_V and st.has(1):
                            act.wait_ge(v_ready, st.count(1, 1, 1))
                            act.wait_ge(v_preset, 1)
                            act.wait_ge(pv_done, st.count(UNITS, -1, UNITS))
                            nc.scalar.copy(v_ext[o][:, :, :, 0:D],
                                           misc_ps[:].rearrange("p (t h d) -> p t h d", t=NT, d=D)).then_inc(v_done, 1)
                        if u == AT_MAX and st.has(1):
                            act.wait_ge(maxT_ready, st.count(1, 1, 1))
                            act.wait_ge(max_written, st.count(16, 0, 16))
                            nc.scalar.copy(maxT[:], maxT_ps).then_inc(maxT_done, 1)
                        if st.has(0):
                            for j in range(GH):
                                act.wait_ge(scored, st.count(TILES, 0, GH * u + j + 1))
                                act.wait_ge(pv_done, st.count(UNITS, 0, u - 1))
                                nc.scalar.activation(probs[:, u % 2, j], score_ps[:, (GH * u + j) % BANKS], ACT.Exp,
                                                     scale=SCALE).then_inc(probs_done, 1)

            @block.tensor
            def _(pe):
                pe.wait_ge(weights_in, 32)
                pe.wait_ge(ident_done, 1)
                for st in steps(pe):
                    p, o = st.slot, (st.slot + 1) % 2

                    def score_for_max(tile):
                        h, t = divmod(tile, NT)
                        if tile % (TILES // 2) == 0:
                            pe.wait_ge(rows_in[tile // (TILES // 2)], st.count(192, 1, 192))
                        pe.wait_ge(max_taken, st.count(TILES, 1, bank_free(tile)))
                        nc.tensor.matmul(max_ps[:, tile % BANKS], q_rows[o][0:MAX_ROW, h, t * 128:(t + 1) * 128],
                                         k_rows[o][0:MAX_ROW, h, :], start=True, stop=True).then_inc(max_scored, 1)

                    def score(u, j):
                        g, t = divmod(u, NT)
                        h = GH * g + j
                        if u == 0 and j == 0:
                            pe.wait_ge(max_rows_in, st.count(16, 0, 16))
                        pe.wait_ge(probs_done, st.count(TILES, 0, bank_free(GH * u + j)))
                        nc.tensor.matmul(score_ps[:, (GH * u + j) % BANKS], k_rows[p][:, h, t * 128:(t + 1) * 128],
                                         q_rows[p][:, h, :], start=True, stop=True).then_inc(scored, 1)

                    def weigh(ahead, u):
                        g, t = divmod(u, NT)
                        pe.wait_ge(probs_done, st.count(TILES, ahead, GH * (u + 1)))
                        if u == 0:
                            pe.wait_ge(v_done, st.count(1, ahead, 1))
                        if t == 0:
                            pe.wait_ge(ctxT_done, st.count(NG, ahead, g))
                        for j in range(GH):
                            last = nc.tensor.matmul(pv_ps[32 * j:32 * j + 32, :], v_ext[(p + ahead) % 2][:, t, GH * g + j],
                                                    probs[:, u % 2, j], start=t == 0, stop=t == NT - 1)
                        last.then_inc(pv_done, 1)

                    def transpose_context(ahead, g):
                        pe.wait_ge(ctxT_done, st.count(NG, ahead, g + 1))
                        for t in range(NT):
                            last = nc.tensor.transpose(misc_ps[:, t * 128:(t + 1) * 128],
                                                       ctxT[:, t * 128:(t + 1) * 128], ident[:])
                        last.then_inc(ctx_ready, 1)

                    tile = 0
                    for u in range(UNITS):
                        if u == AT_CTX and st.has(-1):
                            pe.wait_ge(ctx_done, st.count(NG, -1, NG - 1))
                            if st.has(0):
                                pe.wait_ge(maxT_done, st.count(1, 0, 1))
                            transpose_context(-1, NG - 1)
                        if u % NT == AT_CTX and u > AT_CTX and st.has(0):
                            if u == AT_CTX + NT and st.has(2):
                                pe.wait_ge(q_rest_done, st.count(1, 2, 1))
                            if u == AT_CTX + 2 * NT and st.has(1):
                                pe.wait_ge(v_done, st.count(1, 1, 1))
                            if u == AT_CTX + 3 * NT and st.has(1):
                                pe.wait_ge(maxT_done, st.count(1, 1, 1))
                            pe.wait_ge(ctx_done, st.count(NG, 0, u // NT - 1))
                            transpose_context(0, u // NT - 1)
                        if u == AT_XT and st.has(2):
                            pe.wait_ge(xn_done, st.count(1, 2, 1))
                            pe.wait_ge(maxT_done, st.count(1, 0, 1))
                            pe.wait_ge(ctx_done, st.count(NG, -1, NG))
                            for t in range(NT):
                                last = nc.tensor.transpose(misc_ps[:, t * 128:(t + 1) * 128], xn[:, t], ident[:])
                            last.then_inc(xT_ready, 1)
                        if u == AT_Q and st.has(2):
                            pe.wait_ge(xnT_done, st.count(1, 2, 1))
                            nc.tensor.matmul(misc_ps[:], w_sb[:, 0:H], xnT[:, p], start=True, stop=True).then_inc(q_ready, 1)
                        if u == AT_K and st.has(2):
                            pe.wait_ge(q_rest_done, st.count(1, 2, 1))
                            pe.wait_ge(ctx_done, st.count(NG, 0, 1))
                            nc.tensor.matmul(misc_ps[:], w_sb[:, H:2 * H], xnT[:, p], start=True, stop=True).then_inc(k_ready, 1)
                        if u == AT_V and st.has(1):
                            if st.has(2):
                                pe.wait_ge(k_rest_done, st.count(1, 2, 1))
                            if st.has(0):
                                pe.wait_ge(ctx_done, st.count(NG, 0, 1))
                            for t in range(NT):
                                last = nc.tensor.matmul(misc_ps[:, t * H:(t + 1) * H], xnT[:, o, t * 128:(t + 1) * 128],
                                                        w_sb[:, 2 * H:3 * H], start=True, stop=True)
                            last.then_inc(v_ready, 1)
                        if u == AT_MAX and st.has(1):
                            pe.wait_ge(max_split_done, st.count(1, 1, 1))
                            pe.wait_ge(v_done, st.count(1, 1, 1))
                            if st.has(0):
                                pe.wait_ge(ctx_done, st.count(NG, 0, NG - 2))
                                pe.sem_inc(stood, 1)
                            for t in range(NT):
                                last = nc.tensor.transpose(maxT_ps[:, t * 128:(t + 1) * 128],
                                                           max_split[:, t].rearrange("p j h -> p (j h)"), ident_bf[:])
                            last.then_inc(maxT_ready, 1)

                        for n in range(GH + 1):
                            if n < GH and st.has(0):
                                score(u, n)
                            if n == GH and u == 0 and st.has(-1):
                                weigh(-1, UNITS - 1)
                            if n == GH and u > 0 and st.has(0):
                                weigh(0, u - 1)
                            if n < MAX_TILES[u] and st.has(1):
                                score_for_max(tile)
                                tile += 1

        with ExitStack() as two:
            RING = 3
            ln_stats = sb("ln_stats2", [128, NT, nc.vector.BN_STATS_DIM], FP32, two)
            ln_mv = sb("ln_mv2", [128, NT, 2], FP32, two)
            ln_rstd = sb("ln_rstd2", [128, NT], FP32, two)
            xn = sb("xn2", [128, NT, H], FP32, two)
            xnT_hi = sb("xnT2_hi", [128, RING, S], FP32R, two)
            xnT_lo = sb("xnT2_lo", [128, RING, S], FP32R, two)
            top = sb("top", [128, NT], FP32, two)
            prob = sb("prob", [128, NT, E], FP32, two)
            norm = sb("norm", [128, NT], FP32, two)
            beats = sb("beats", [128, NT, E, E], FP32, two)
            ties = sb("ties", [128, NT, E, E], FP32, two)
            rank = sb("rank", [128, NT, E], FP32, two)
            route = sb("route", [128, E, NT], FP32, two)
            routeT = sb("routeT", [E * NT, 128], FP32, two)
            route_all = sb("route_all", [128, RING, E, S], FP32, two)
            gate_tanh = sb("gate_tanh", [128, 2, S], FP32, two)
            gate_act = sb("gate_act", [128, 2, S], FP32, two)
            gate_wgt = sb("gate_wgt", [128, 2, S], FP32, two)
            hidden = sb("hidden", [128, 3, S], FP32, two)
            yT = sb("yT", [128, S], FP32, two)
            out_sb = sb("out_sb", [128, RING, NT, H], FP32, two)

            gate_ps = ps("gate_ps", [128, 2, S], FP32, two)
            up_ps = ps("up_ps", [128, 2, S], FP32, two)
            y_ps = ps("y_ps", [128, S], FP32, two)
            xT_ps = ps("xT_ps", [128, S], FP32, two)
            route_ps = ps("route_ps", [128, 512], FP32, two)
            yt_ps = ps("yt_ps", [128, S], FP32, two)
            logits = route_ps[:, 0:NT * E].rearrange("p (t e) -> p t e", t=NT)
            routeT_ps = route_ps[0:E * NT, 128:256]

            dve_link = sem("dve_link", two)
            stats_done = sem("stats2_done", two)
            mv_done = sem("mv2_done", two)
            var_done = sem("var2_done", two)
            rstd_done = sem("rstd2_done", two)
            xn_done = sem("xn2_done", two)
            xT_ready = sem("xT2_ready", two)
            xnT_hi_done = sem("xnT2_hi_done", two)
            xnT_lo_done = sem("xnT2_lo_done", two)
            logits_ready = sem("logits_ready", two)
            logits_shifted = sem("logits_shifted", two)
            exp_done = sem("exp_done", two)
            route_done = sem("route_done", two)
            routeT_ready = sem("routeT_ready", two)
            routeT_done = sem("routeT_done", two)
            route_written = sem("route_written", two)
            route_in = [sem(f"route_in{i}", two) for i in range(RING)]
            gate_ready = sem("gate_ready", two)
            up_ready = sem("up_ready", two)
            tanh_done = sem("tanh_done", two)
            gate_act_done = sem("gate_act_done", two)
            gate_wgt_done = sem("gate_wgt_done", two)
            hidden_done = sem("hidden_done", two)
            down_done = sem("down_done", two)
            yT_done = sem("yT_done", two)
            yt_ready = sem("yt_ready", two)
            out_done = sem("out_done", two)
            stored = [sem(f"stored{i}", two) for i in range(RING)]

            LAG = 2
            AT_CENTRE, AT_XT2, AT_LOGITS, AT_TOP, AT_ROUTE, AT_Y, AT_YT = 1, 2, 4, 5, 7, 2, 4
            LINKS = 18

            block = two.enter_context(nc.Block())

            def steps2(engine):
                return walk(engine, (-2, -1, 0), RING, (B - 4) // RING, range(B - 3, B + 1), B)

            def hidden_slot(st, ahead, e):
                return (((st.slot + ahead) % RING) * E + e) % 3


            @block.sync
            def _(sp):
                for i in range(RING):
                    sp.sem_inc(stored[i], 16)
                for st in steps2(sp):
                    p = st.slot
                    if st.has(-1):
                        o = (p + RING - 1) % RING
                        sp.wait_ge(out_done, st.count(1, -1, 2))
                        sp.sem_inc(stood, 1)
                        sp.dma_start(out_v[bass.ds(st.number - 1, 1)].rearrange("o p t h -> (o p) t h"),
                                     out_sb[:, o]).then_inc(stored[o], 16)
                    if st.has(2):
                        o = (p + 2) % RING
                        sp.wait_ge(routeT_done, st.count(1, 2, 1))
                        sp.dma_start(route_scratch[o].rearrange("e t p -> (e t) p"), routeT[:]).then_inc(route_written, 16)
                        sp.wait_ge(route_written, st.count(16, 2, 16))
                        sp.sem_inc(stood, 1)
                        sp.wait_ge(gate_wgt_done, st.count(E, -1, E))
                        sp.dma_start(route_all[:, o].rearrange("p e s -> p (e s)"),
                                     route_scratch[o].rearrange("e t p -> (e t p)").partition_broadcast(128)
                                     ).then_inc(route_in[o], 16)
                for i in range(RING):
                    sp.wait_ge(stored[i], 16 + 16 * len(range(i, B, RING)))

            @block.gpsimd
            def _(pool):
                for st in steps2(pool):
                    p = st.slot
                    if st.has(2):
                        pool.wait_ge(mv_done, st.count(1, 2, 1))
                        pool.sem_inc(stood, 1)
                        pool.wait_ge(xn_done, st.count(1, 1, 1))
                        pool.sem_inc(stood, 1)
                        nc.gpsimd.tensor_scalar(ln_var[:], ln_mv[:, :, 1], LN_EPS, None, ALU.add).then_inc(var_done, 1)
                        pool.wait_ge(var_done, st.count(1, 2, 1))
                        pool.sem_inc(stood, 1)
                        nc.gpsimd.tensor_tensor(ln_rstd[:], ln_var[:], minus_half[:], ALU.pow).then_inc(rstd_done, 1)
                    for e in range(E):
                        if st.has(0):
                            n = e % 2
                            if e == 0:
                                pool.wait_ge(route_in[st.buffer(0)], st.loads(0))
                            pool.wait_ge(gate_act_done, st.count(E, 0, e + 1))
                            pool.sem_inc(stood, 1)
                            pool.wait_ge(hidden_done, st.count(E, 0, e - 1))
                            pool.sem_inc(stood, 1)
                            nc.gpsimd.tensor_tensor(gate_wgt[:, n], gate_act[:, n], route_all[:, p, e],
                                                    ALU.mult).then_inc(gate_wgt_done, 1)

            @block.vector
            def _(dve):
                dve.sem_inc(out_done, 1)
                for st in steps2(dve):
                    p = st.slot
                    front = (p + 2) % RING
                    links = [0]

                    def link(instruction):
                        instruction.then_inc(dve_link, 1)
                        links[0] += 1
                        dve.wait_ge(dve_link, st.count(LINKS, 2, links[0]))

                    def normalise():
                        at = (st.number + 2) * S
                        tiles = [x_all[:, bass.ds(at + t * H, H)] for t in range(NT)]
                        for t in range(NT):
                            last = nc.vector.bn_stats(ln_stats[:, t], tiles[t])
                        last.then_inc(stats_done, 1)
                        dve.wait_ge(stats_done, st.count(1, 2, 1))
                        dve.sem_inc(stood, 1)
                        for t in range(NT - 1):
                            nc.vector.bn_aggr(ln_mv[:, t], ln_stats[:, t])
                        nc.vector.bn_aggr(ln_mv[:, NT - 1], ln_stats[:, NT - 1]).then_inc(mv_done, 1)

                    def centre():
                        at = (st.number + 2) * S
                        tiles = [x_all[:, bass.ds(at + t * H, H)] for t in range(NT)]
                        dve.wait_ge(rstd_done, st.count(1, 2, 1))
                        dve.wait_ge(xT_ready, st.count(1, 1, 1))
                        for t in range(NT):
                            last = nc.vector.tensor_scalar(xn[:, t], tiles[t], ln_mv[:, t, 0:1], ln_rstd[:, t:t + 1],
                                                           ALU.subtract, ALU.mult)
                        last.then_inc(xn_done, 1)

                    def spread(v):
                        return v[:].unsqueeze(2).to_broadcast([128, NT, E])

                    def softmax_shift():
                        dve.wait_ge(logits_ready, st.count(1, 2, 1))
                        link(nc.vector.reduce_max(top[:], logits, AX.X))
                        nc.vector.tensor_tensor(prob[:], logits, spread(top), ALU.subtract).then_inc(logits_shifted, 1)

                    def softmax_divide():
                        dve.wait_ge(exp_done, st.count(1, 2, 1))
                        link(nc.vector.reduce_sum(norm[:], prob[:], AX.X))
                        link(nc.vector.reciprocal(norm[:], norm[:]))
                        link(nc.vector.tensor_tensor(prob[:], prob[:], spread(norm), ALU.mult))

                    def top_two():
                        mine = prob[:].unsqueeze(3).to_broadcast([128, NT, E, E])
                        other = prob[:].unsqueeze(2).to_broadcast([128, NT, E, E])
                        nc.vector.tensor_tensor(beats[:], other, mine, ALU.is_gt)
                        link(nc.vector.tensor_tensor(ties[:], other, mine, ALU.is_equal))
                        link(nc.vector.tensor_tensor(ties[:], ties[:], earlier[:], ALU.mult))
                        link(nc.vector.tensor_tensor(beats[:], beats[:], ties[:], ALU.add))
                        link(nc.vector.reduce_sum(rank[:], beats[:], AX.X))
                        link(nc.vector.tensor_scalar(rank[:], rank[:], 1.5, None, ALU.is_lt))
                        link(nc.vector.tensor_tensor(prob[:], prob[:], rank[:], ALU.mult))
                        for last_time in (False, True):
                            link(nc.vector.reduce_sum(norm[:], prob[:], AX.X))
                            link(nc.vector.tensor_scalar(norm[:], norm[:], TOP_EPS, None, ALU.add))
                            if last_time:
                                link(nc.vector.tensor_scalar(norm[:], norm[:], 2.0, None, ALU.mult))
                            link(nc.vector.reciprocal(norm[:], norm[:]))
                            if not last_time:
                                link(nc.vector.tensor_tensor(prob[:], prob[:], spread(norm), ALU.mult))
                        assert links[0] == LINKS
                        dve.wait_ge(routeT_ready, st.count(1, 1, 1))
                        nc.vector.tensor_tensor(route[:].rearrange("p e t -> p t e"), prob[:], spread(norm),
                                                ALU.mult).then_inc(route_done, 1)

                    def hide(ahead, e):
                        dve.wait_ge(gate_wgt_done, st.count(E, ahead, e + 1))
                        dve.wait_ge(up_ready, st.count(E, ahead, e + 1))
                        dve.wait_ge(down_done, st.count(E, ahead, e - 2))
                        nc.vector.tensor_tensor(hidden[:, hidden_slot(st, ahead, e)], up_ps[:, e % 2], gate_wgt[:, e % 2],
                                                ALU.mult).then_inc(hidden_done, 1)

                    if st.has(2):
                        normalise()
                    for e in range(E):
                        if e == AT_CENTRE and st.has(2):
                            centre()
                        if st.has(0):
                            dve.wait_ge(tanh_done, st.count(E, 0, e + 1))
                            dve.wait_ge(gate_wgt_done, st.count(E, 0, e - 1))
                            nc.vector.scalar_tensor_tensor(out=gate_act[:, e % 2], in0=gate_tanh[:, e % 2], scalar=1.0,
                                                           in1=gate_ps[:, e % 2], op0=ALU.add,
                                                           op1=ALU.mult).then_inc(gate_act_done, 1)
                        if e == 0 and st.has(-1):
                            hide(-1, E - 1)
                        if e > 0 and st.has(0):
                            hide(0, e - 1)
                        if st.has(2):
                            if e == AT_XT2:
                                dve.wait_ge(xnT_hi_done, st.count(1, 2, 1))
                                nc.vector.tensor_tensor(xnT_lo[:, front], xT_ps[:], xnT_hi[:, front].bitcast(FP32),
                                                        ALU.subtract).then_inc(xnT_lo_done, 1)
                            if e == AT_LOGITS:
                                softmax_shift()
                                softmax_divide()
                            if e == AT_TOP:
                                top_two()
                        if e == AT_YT and st.has(-1):
                            o = (p + RING - 1) % RING
                            dve.wait_ge(yt_ready, st.count(1, -1, 2))
                            dve.wait_ge(stored[st.buffer(-1)], st.loads(-1))
                            nc.vector.tensor_tensor(out_sb[:, o].rearrange("p t h -> p (t h)"), yt_ps[:],
                                                    x_all[:, bass.ds((st.number - 1) * S, S)], ALU.add).then_inc(out_done, 1)

            @block.scalar
            def _(act):
                for st in steps2(act):
                    p = st.slot
                    front = (p + 2) % RING
                    for e in range(E):
                        if e == AT_Y and st.has(-1):
                            act.wait_ge(down_done, st.count(E, -1, E))
                            act.wait_ge(yt_ready, st.count(1, -2, 2))
                            nc.scalar.copy(yT[:], y_ps[:]).then_inc(yT_done, 1)
                        if e == AT_XT2 and st.has(2):
                            act.wait_ge(xT_ready, st.count(1, 2, 1))
                            act.wait_ge(up_ready, st.count(E, -1, E))
                            nc.scalar.copy(xnT_hi[:, front], xT_ps[:]).then_inc(xnT_hi_done, 1)
                        if e == AT_ROUTE and st.has(2):
                            act.wait_ge(routeT_ready, st.count(1, 2, 1))
                            act.wait_ge(route_written, st.count(16, 1, 16))
                            nc.scalar.copy(routeT[:], routeT_ps).then_inc(routeT_done, 1)
                        if st.has(0):
                            act.wait_ge(gate_ready, st.count(E, 0, e + 1))
                            act.wait_ge(gate_act_done, st.count(E, 0, e - 1))
                            nc.scalar.activation(gate_tanh[:, e % 2], gate_ps[:, e % 2], ACT.Tanh,
                                                 scale=0.5).then_inc(tanh_done, 1)
                        if e == AT_LOGITS and st.has(2):
                            act.wait_ge(logits_shifted, st.count(1, 2, 1))
                            nc.scalar.activation(prob[:], prob[:], ACT.Exp).then_inc(exp_done, 1)

            @block.tensor
            def _(pe):
                pe.sem_inc(yt_ready, 1)
                for st in steps2(pe):
                    p = st.slot
                    front = (p + 2) % RING

                    def project(where, e, columns):
                        nc.tensor.matmul(where, w_gu_hi[:, e, columns], xnT_hi[:, p], start=True, stop=False)
                        nc.tensor.matmul(where, w_gu_hi[:, e, columns], xnT_lo[:, p], start=False, stop=False)
                        return nc.tensor.matmul(where, w_gu_lo[:, e, columns], xnT_hi[:, p], start=False, stop=True)

                    def down(ahead, e):
                        pe.wait_ge(hidden_done, st.count(E, ahead, e + 1))
                        if e == 0:
                            pe.wait_ge(yT_done, st.count(1, ahead - 1, 1))
                        nc.tensor.matmul(y_ps[:], w_down[:, e], hidden[:, hidden_slot(st, ahead, e)], start=e == 0,
                                         stop=e == E - 1).then_inc(down_done, 1)

                    for e in range(E):
                        if e == AT_XT2 and st.has(2):
                            pe.wait_ge(xn_done, st.count(1, 2, 1))
                            pe.wait_ge(xnT_lo_done, st.count(1, 1, 1))
                            for t in range(NT):
                                last = nc.tensor.transpose(xT_ps[:, t * 128:(t + 1) * 128], xn[:, t], ident[:])
                            last.then_inc(xT_ready, 1)
                        if e == AT_LOGITS and st.has(2):
                            pe.wait_ge(xnT_lo_done, st.count(1, 2, 1))
                            pe.wait_ge(routeT_done, st.count(1, 1, 1))
                            for t in range(NT):
                                tokens = slice(t * 128, (t + 1) * 128)
                                where = route_ps[:, t * E:(t + 1) * E]
                                nc.tensor.matmul(where, xnT_hi[:, front, tokens], w_gate_hi[:], start=True, stop=False)
                                nc.tensor.matmul(where, xnT_hi[:, front, tokens], w_gate_lo[:], start=False, stop=False)
                                last = nc.tensor.matmul(where, xnT_lo[:, front, tokens], w_gate_hi[:],
                                                        start=False, stop=True)
                            last.then_inc(logits_ready, 1)
                        if e == AT_ROUTE and st.has(2):
                            pe.wait_ge(route_done, st.count(1, 2, 1))
                            nc.tensor.transpose(routeT_ps, route[:].rearrange("p e t -> p (e t)"), ident[:]).then_inc(routeT_ready, 1)
                        if e == AT_YT and st.has(-1):
                            pe.wait_ge(yT_done, st.count(1, -1, 1))
                            pe.wait_ge(out_done, st.count(1, -2, 2))
                            for t in range(NT):
                                last = nc.tensor.transpose(yt_ps[:, t * 128:(t + 1) * 128], yT[:, t * 128:(t + 1) * 128], ident[:])
                            last.then_inc(yt_ready, 1)
                        if st.has(0):
                            pe.wait_ge(gate_act_done, st.count(E, 0, e - 1))
                            project(gate_ps[:, e % 2], e, slice(0, H)).then_inc(gate_ready, 1)
                            pe.wait_ge(hidden_done, st.count(E, 0, e - 1))
                            project(up_ps[:, e % 2], e, slice(H, 2 * H)).then_inc(up_ready, 1)
                        if e < LAG and st.has(-1):
                            down(-1, E - LAG + e)
                        if e >= LAG and st.has(0):
                            down(0, e - LAG)


_INS = ['L0_attn_embeddings', 'L0_attn_w_qkv', 'L0_ffn_gate_w', 'L0_ffn_gate_up_proj', 'L0_ffn_down_proj']
_OUTS = [((16, 512, 128), 'float32')]


def kernel(**inputs):
    import numpy as _np
    import concourse.bacc as _bacc
    from concourse import mybir as _mybir
    from concourse.bass_utils import run_bass_kernel_spmd as _run

    nc = _bacc.Bacc("TRN2", target_bir_lowering=False, num_devices=1)
    arrays, args = {}, []
    for name in _INS + ['identity']:
        a = _np.eye(128, dtype=_np.float32) if name == 'identity' else _np.asarray(inputs[name])
        if name == 'L0_ffn_gate_w':
            a = a.T
        a = _np.ascontiguousarray(a)
        arrays[f"in_{name}_dram"] = a
        args.append(nc.dram_tensor(f"in_{name}_dram", a.shape, _mybir.dt.from_np(a.dtype), kind="ExternalInput").ap())
    for i, (shape, dtype) in enumerate(_OUTS):
        dt = _mybir.dt.from_np(_np.dtype(dtype))
        args.append(nc.dram_tensor(f"out_{i}_dram", shape, dt, kind="ExternalOutput").ap())
    attention_moe_kernel(nc, *args)
    r = _run(nc, [arrays], core_ids=[0])
    got = tuple(r.results[0][f"out_{i}_dram"] for i in range(len(_OUTS)))
    return got[0]
```

```python
import concourse.bass as bass
from concourse import mybir
from contextlib import ExitStack

FP32 = mybir.dt.float32
BF16 = mybir.dt.bfloat16
FP32R = mybir.dt.float32r
ALU = mybir.AluOpType
ACT = mybir.ActivationFunctionType
AX = mybir.AxisListType


class Step:

    def __init__(self, number, passes, unroll, least, most, batches):
        self.number, self.passes, self.unroll = number, passes, unroll
        self.least, self.most, self.batches = least, most, batches
        self.slot = least % unroll

    def buffer(self, ahead):
        return (self.least + ahead) % self.unroll

    def loads(self, ahead):
        return self.passes * 16 + 16 * ((self.least + ahead) // self.unroll + 1)

    def has(self, ahead):
        first, last = self.least + ahead, self.most + ahead
        assert (0 <= first and last < self.batches) or first == last or last < 0 or first >= self.batches
        return 0 <= first and last < self.batches

    def count(self, per_batch, ahead, k):
        least = per_batch * (self.least + ahead) + k
        if self.least == self.most:
            return max(least, 0)
        assert least > 0
        return self.number * per_batch + (per_batch * ahead + k)


def walk(engine, before, unroll, loops, after, batches):
    for s in before:
        yield Step(s, 0, unroll, s, s, batches)
    first = before[-1] + 1
    with engine.Fori(0, loops) as i:
        for k in range(first, first + unroll):
            yield Step(i * unroll + k, i, unroll, k, k + (loops - 1) * unroll, batches)
    for s in after:
        yield Step(s, 0, unroll, s, s, batches)


def attention_moe_kernel(
    nc: bass.Bass,
    x: bass.AP,
    w_qkv: bass.AP,
    gate_w: bass.AP,
    gate_up_proj: bass.AP,
    down_proj: bass.AP,
    identity: bass.AP,
    out: bass.AP,
):
    B, S, H = x.shape
    E = gate_w.shape[1]
    NH = 16
    D = H // NH
    NT = S // 128
    LN_EPS = 1e-5
    TOP_EPS = 1e-9
    SCALE = float(H) ** -0.5

    Q_PARTS = (0, 0, 0, 1, 1, 2)
    K_PARTS = (0, 1, 2, 0, 1, 0)
    PARTS = 3
    MAX_ROW = 96
    GH = 4
    NG = NH // GH
    UNITS = NG * NT
    HALF = NH // 2
    TILES = NH * NT
    BANKS = 3

    def bank_free(tile):
        if tile >= BANKS:
            return tile - BANKS + 1
        before = [n for n in range(TILES) if n % BANKS == tile]
        return before[-1] + 1 - TILES

    MAX_TILES = [TILES // UNITS] * UNITS
    assert sum(MAX_TILES) == TILES
    AT_CTX, AT_XT, AT_Q, AT_K, AT_V = 3, 4, 6, 8, 10
    AT_MAX = (12, 1)
    AT_STATS = 1

    x_v = x.rearrange("b (t p) h -> b p t h", p=128)
    out_v = out.rearrange("b (t p) h -> b p t h", p=128)
    q_scratch = nc.dram_tensor("q_scratch", (2, PARTS, NH, D, S), BF16, kind="Internal").ap()
    k_scratch = nc.dram_tensor("k_scratch", (2, PARTS, NH, D, S), BF16, kind="Internal").ap()
    max_scratch = nc.dram_tensor("max_scratch", (2, 2, PARTS, HALF, S), BF16, kind="Internal").ap()
    route_scratch = nc.dram_tensor("route_scratch", (3, E, NT, 128), FP32, kind="Internal").ap()

    with ExitStack() as whole:
        def sem(name, stack=whole):
            return stack.enter_context(nc.semaphore(name))

        def sb(name, shape, dtype, stack=whole):
            return stack.enter_context(nc.sbuf_tensor(name, shape, dtype))

        def ps(name, shape, dtype, stack=whole):
            return stack.enter_context(nc.psum_tensor(name, shape, dtype))

        stood = sem("stood")
        x_all = sb("x_all", [128, B * S], FP32)
        ident = sb("ident", [128, 128], FP32)
        w_gu = sb("w_gu", [128, E, 2 * H], FP32)
        w_down = sb("w_down", [128, E, H], FP32)
        w_gate = sb("w_gate", [128, E], FP32)
        w_gu_hi = sb("w_gu_hi", [128, E, 2 * H], FP32R)
        w_gu_lo = sb("w_gu_lo", [128, E, 2 * H], FP32R)
        w_gate_hi = sb("w_gate_hi", [128, E], FP32R)
        w_gate_lo = sb("w_gate_lo", [128, E], FP32R)
        earlier = sb("earlier", [128, NT, E, E], FP32)

        ln_var = sb("ln_var", [128, NT], FP32)
        minus_half = sb("minus_half", [128, NT], FP32)

        with ExitStack() as one:
            w_sb = sb("w_sb", [128, 3 * H], FP32, one)
            ident_bf = sb("ident_bf", [128, 128], BF16, one)
            xin = sb("xin", [128, 2, NT, H], FP32, one)
            ln_stats = sb("ln_stats", [128, NT, nc.vector.BN_STATS_DIM], FP32, one)
            ln_mv = sb("ln_mv", [128, 2, NT, 2], FP32, one)
            ln_rstd = sb("ln_rstd", [128, 2, NT], FP32, one)
            xn = sb("xn", [128, NT, H], FP32, one)
            xnT = sb("xnT", [128, 2, S], FP32, one)
            q_split = sb("q_split", [128, PARTS, S], BF16, one)
            k_split = sb("k_split", [128, PARTS, S], BF16, one)
            q_rest = sb("q_rest", [128, S], FP32, one)
            k_rest = sb("k_rest", [128, S], FP32, one)
            q_rows = [sb(f"q_rows{i}", [128, NH, S], BF16, one) for i in range(2)]
            k_rows = [sb(f"k_rows{i}", [128, NH, S], BF16, one) for i in range(2)]
            v_ext = [sb(f"v_ext{i}", [128, NT, NH, 32], FP32, one) for i in range(2)]
            neg_max = sb("neg_max", [128, 2, NT, HALF], FP32, one)
            max_rest = sb("max_rest", [128, NT, HALF], FP32, one)
            max_split = sb("max_split", [128, 2, NT, PARTS, HALF], BF16, one)
            maxT = sb("maxT", [PARTS * HALF, 2, S], BF16, one)
            probs = sb("probs", [128, 2, GH, S], FP32, one)
            ctxT = sb("ctxT", [128, S], FP32, one)
            inv_sum = sb("inv_sum", [128, NT, GH], FP32, one)
            ctx_out = sb("ctx_out", [128, 2, NT, H], FP32, one)

            score_ps = ps("score_ps", [128, BANKS, S], FP32, one)
            max_ps = ps("max_ps", [128, BANKS, S], FP32, one)
            pv_ps = ps("pv_ps", [128, S], FP32, one)
            misc_ps = ps("misc_ps", [128, 512], FP32, one)
            maxT_ps = misc_ps[0:PARTS * HALF, 0:S // 2].bitcast(BF16)

            weights_in = sem("weights_in", one)
            moe_weights_in = sem("moe_weights_in", one)
            x_all_in = sem("x_all_in", one)
            w_hi_done = sem("w_hi_done", one)
            xin_in = [sem(f"xin_in{i}", one) for i in range(2)]
            earlier_zeroed = sem("earlier_zeroed", one)
            q_rows_preset = sem("q_rows_preset", one)
            k_rows_preset = sem("k_rows_preset", one)
            v_zeroed = sem("v_zeroed", one)
            v_preset = sem("v_preset", one)
            ident_done = sem("ident_done", one)
            stats_done = sem("stats_done", one)
            mv_done = sem("mv_done", one)
            var_done = sem("var_done", one)
            rstd_done = sem("rstd_done", one)
            xn_done = sem("xn_done", one)
            xT_ready = sem("xT_ready", one)
            xnT_done = sem("xnT_done", one)
            q_ready = sem("q_ready", one)
            k_ready = sem("k_ready", one)
            v_ready = sem("v_ready", one)
            q_hi_done = sem("q_hi_done", one)
            k_hi_done = sem("k_hi_done", one)
            q_rest_done = sem("q_rest_done", one)
            k_rest_done = sem("k_rest_done", one)
            q_mid_done = sem("q_mid_done", one)
            k_mid_done = sem("k_mid_done", one)
            q_lo_done = sem("q_lo_done", one)
            k_lo_done = sem("k_lo_done", one)
            q_written = sem("q_written", one)
            k_written = sem("k_written", one)
            rows_in = [sem(f"rows_in{i}", one) for i in range(2)]
            v_done = sem("v_done", one)
            max_scored = sem("max_scored", one)
            max_taken = sem("max_taken", one)
            max_hi_done = sem("max_hi_done", one)
            max_rest_done = sem("max_rest_done", one)
            max_mid_done = sem("max_mid_done", one)
            max_split_done = sem("max_split_done", one)
            maxT_ready = sem("maxT_ready", one)
            maxT_done = sem("maxT_done", one)
            max_written = sem("max_written", one)
            max_rows_in = sem("max_rows_in", one)
            scored = sem("scored", one)
            probs_done = sem("probs_done", one)
            pv_done = sem("pv_done", one)
            ctxT_done = sem("ctxT_done", one)
            ctx_ready = sem("ctx_ready", one)
            inv_done = sem("inv_done", one)
            ctx_done = sem("ctx_done", one)
            x1_done = sem("x1_done", one)

            block = one.enter_context(nc.Block())

            def steps(engine):
                return walk(engine, (-2, -1, 0), 2, (B - 4) // 2, range(B - 3, B + 1), B)

            @block.sync
            def _(sp):
                def load_x(b):
                    sp.dma_start(xin[:, b % 2], x_v[b]).then_inc(xin_in[b % 2], 16)

                load_x(0)
                sp.dma_start(ident[:], identity).then_inc(weights_in, 16)
                sp.dma_start(w_sb[:], w_qkv).then_inc(weights_in, 16)
                for st in steps(sp):
                    p = st.slot
                    if st.has(3):
                        sp.wait_ge(xn_done, st.count(1, 1, 1))
                        sp.dma_start(xin[:, (p + 1) % 2], x_v[bass.ds(st.number + 3, 1)].rearrange(
                            "o p t h -> (o p) t h")).then_inc(xin_in[(p + 1) % 2], 16)

                    def load_max(ahead, half):
                        o = (p + ahead) % 2
                        sp.wait_ge(maxT_done, st.count(2, ahead, half + 1))
                        sp.dma_start(max_scratch[o, half].rearrange("j h s -> (j h) s"),
                                     maxT[:, half]).then_inc(max_written, 16)
                        sp.wait_ge(max_written, st.count(32, ahead, 16 * (half + 1)))
                        sp.sem_inc(stood, 1)
                        sp.wait_ge(max_rows_in, st.count(32, ahead, 16 * half))
                        sp.dma_start(q_rows[o][MAX_ROW:MAX_ROW + PARTS, half * HALF:(half + 1) * HALF, :],
                                     max_scratch[o, half]).then_inc(max_rows_in, 16)

                    if st.has(0):
                        load_max(0, 1)
                    if st.least == st.most == -2:
                        sp.dma_start(x_all[:].rearrange("p (b t h) -> p b t h", b=B, t=NT),
                                     x_v.rearrange("b p t h -> p b t h")).then_inc(x_all_in, 16)
                        sp.dma_start(w_gu[:], gate_up_proj.rearrange("e h q -> h e q")).then_inc(moe_weights_in, 16)
                        sp.dma_start(w_down[:], down_proj.rearrange("e q h -> q e h")).then_inc(moe_weights_in, 16)
                        sp.dma_start(w_gate[:], gate_w).then_inc(moe_weights_in, 16)
                    if st.has(2):
                        for split, scratch, lo_done, written in (
                                (q_split, q_scratch, q_lo_done, q_written),
                                (k_split, k_scratch, k_lo_done, k_written)):
                            sp.wait_ge(lo_done, st.count(1, 2, 1))
                            for j in range(PARTS):
                                sp.dma_start(scratch[p, j].rearrange("h d s -> (h d) s"),
                                             split[:, j]).then_inc(written, 16)
                        sp.wait_ge(q_written, st.count(48, 2, 48))
                        sp.wait_ge(k_written, st.count(48, 2, 48))

                    def load_rows(half):
                        if st.has(0):
                            sp.wait_ge(scored, st.count(TILES, 0, TILES // 2 * (half + 1)))
                        sp.wait_ge(rows_in[half], st.count(192, 1, 192))
                        h = slice(half * HALF, (half + 1) * HALF)
                        for rows, scratch, parts in ((q_rows, q_scratch, Q_PARTS), (k_rows, k_scratch, K_PARTS)):
                            for n, j in enumerate(parts):
                                sp.dma_start(rows[p][n * D:(n + 1) * D, h, :],
                                             scratch[p, j, h].rearrange("h d s -> d h s")).then_inc(rows_in[half], 16)

                    if st.has(2):
                        if st.least == st.most and st.least < 0:
                            sp.wait_ge(q_rows_preset, st.least + 3)
                            sp.wait_ge(k_rows_preset, st.least + 3)
                        load_rows(0)
                    if st.has(1):
                        load_max(1, 0)
                    if st.has(2):
                        load_rows(1)
                sp.wait_ge(moe_weights_in, 48)

            @block.gpsimd
            def _(pool):
                def lay_ones(rows):
                    nc.gpsimd.memset(rows[:].rearrange("p h s -> p (h s)").bitcast(FP32),
                                     1.0019378662109375).then_inc(k_rows_preset, 1)

                nc.gpsimd.memset(minus_half[:], -0.5).then_inc(x1_done, 1)
                lay_ones(k_rows[0])
                nc.gpsimd.memset(earlier[:], 0.0).then_inc(earlier_zeroed, 1)
                pool.wait_ge(earlier_zeroed, 1)
                for e in range(1, E):
                    nc.gpsimd.memset(earlier[:, :, e, 0:e], 1.0)
                for st in steps(pool):
                    p = st.slot
                    first = st.least == st.most == -2
                    if st.least == st.most == B - 3:
                        pool.wait_ge(moe_weights_in, 48)
                        nc.gpsimd.tensor_copy(w_gu_hi[:], w_gu[:])
                        nc.gpsimd.tensor_copy(w_gate_hi[:], w_gate[:]).then_inc(w_hi_done, 1)
                        pool.wait_ge(w_hi_done, 1)
                        nc.gpsimd.tensor_tensor(w_gu_lo[:], w_gu[:], w_gu_hi[:].bitcast(FP32), ALU.subtract)
                        nc.gpsimd.tensor_tensor(w_gate_lo[:], w_gate[:], w_gate_hi[:].bitcast(FP32), ALU.subtract)
                    if st.has(2):
                        pool.wait_ge(mv_done, st.count(1, 2, 1))
                        pool.sem_inc(stood, 1)
                        nc.gpsimd.tensor_scalar(ln_var[:], ln_mv[:, p, :, 1], LN_EPS, None, ALU.add).then_inc(var_done, 1)
                        pool.wait_ge(var_done, st.count(1, 2, 1))
                        pool.sem_inc(stood, 1)
                        nc.gpsimd.tensor_tensor(ln_rstd[:, p], ln_var[:], minus_half[:], ALU.pow).then_inc(rstd_done, 1)
                    if st.has(2) and not first:
                        pool.wait_ge(rstd_done, st.count(1, 2, 1))
                        pool.sem_inc(stood, 1)
                        pool.wait_ge(xT_ready, st.count(1, 1, 1))
                        pool.sem_inc(stood, 1)
                        for t in range(NT):
                            last = nc.gpsimd.tensor_scalar(xn[:, t], xin[:, p, t], ln_mv[:, p, t, 0:1],
                                                           ln_rstd[:, p, t:t + 1], ALU.subtract, ALU.mult)
                        last.then_inc(xn_done, 1)
                    if st.has(-1):
                        o = (p + 1) % 2
                        if st.least == 1 or st.least == st.most:
                            pool.wait_ge(x_all_in, 16)
                        pool.wait_ge(ctx_done, st.count(NG, -1, NG))
                        pool.sem_inc(stood, 1)
                        here = x_all[:, bass.ds((st.number - 1) * S, S)]
                        nc.gpsimd.tensor_tensor(here, here, ctx_out[:, o].rearrange("p t h -> p (t h)"),
                                                ALU.add).then_inc(x1_done, 1)
                    if st.has(2) and not first:
                        for rest, split, rest_done, mid_done, lo_done, written in (
                                (q_rest, q_split, q_rest_done, q_mid_done, q_lo_done, q_written),
                                (k_rest, k_split, k_rest_done, k_mid_done, k_lo_done, k_written)):
                            pool.wait_ge(rest_done, st.count(1, 2, 1))
                            pool.sem_inc(stood, 1)
                            pool.wait_ge(written, st.count(48, 1, 48))
                            pool.sem_inc(stood, 1)
                            nc.gpsimd.tensor_copy(split[:, 1], rest[:]).then_inc(mid_done, 1)
                            pool.wait_ge(mid_done, st.count(1, 2, 1))
                            pool.sem_inc(stood, 1)
                            nc.gpsimd.tensor_tensor(split[:, 2], rest[:], split[:, 1],
                                                    ALU.subtract).then_inc(lo_done, 1)
                    if first:
                        lay_ones(k_rows[1])

            @block.vector
            def _(dve):
                nc.vector.memset(q_rows[0][:], 0.0).then_inc(q_rows_preset, 1)
                for st in steps(dve):
                    p, o = st.slot, (st.slot + 1) % 2
                    first = st.least == st.most == -2

                    def normal_stats():
                        dve.wait_ge(xin_in[st.buffer(2)], st.loads(2))
                        dve.wait_ge(mv_done, st.count(1, 1, 1))
                        for t in range(NT):
                            last = nc.vector.bn_stats(ln_stats[:, t], xin[:, p, t])
                        last.then_inc(stats_done, 1)
                        dve.wait_ge(xn_done, st.count(1, 0, 1))
                        dve.wait_ge(stats_done, st.count(1, 2, 1))
                        dve.sem_inc(stood, 1)
                        for t in range(NT):
                            last = nc.vector.bn_aggr(ln_mv[:, p, t], ln_stats[:, t])
                        last.then_inc(mv_done, 1)

                    def rest(split, rest_sb, hi_done, rest_done, mid_done, lo_done):
                        dve.wait_ge(hi_done, st.count(1, 2, 1))
                        dve.wait_ge(lo_done, st.count(1, 1, 1))
                        nc.vector.tensor_tensor(rest_sb[:], misc_ps[:], split[:, 0],
                                                ALU.subtract).then_inc(rest_done, 1)
                        if first:
                            dve.wait_ge(rest_done, 1)
                            nc.vector.tensor_copy(split[:, 1], rest_sb[:]).then_inc(mid_done, 1)
                            dve.wait_ge(mid_done, 1)
                            nc.vector.tensor_tensor(split[:, 2], rest_sb[:], split[:, 1],
                                                    ALU.subtract).then_inc(lo_done, 1)

                    def normal_ctx(ahead, g):
                        out_p = (p + ahead) % 2
                        view = misc_ps[:].rearrange("p (t j i) -> p t j i", t=NT, j=GH)
                        dve.wait_ge(ctx_ready, st.count(NG, ahead, g + 1))
                        dve.wait_ge(ctx_done, st.count(NG, ahead, g))
                        nc.vector.reciprocal(inv_sum[:], view[:, :, :, D]).then_inc(inv_done, 1)
                        dve.wait_ge(inv_done, st.count(NG, ahead, g + 1))
                        if g == 0:
                            dve.wait_ge(x1_done, st.count(1, ahead - 2, 2))
                        nc.vector.tensor_tensor(
                            ctx_out[:, out_p].rearrange("p t (g j i) -> p t g j i", g=NG, j=GH)[:, :, g],
                            view[:, :, :, 0:D], inv_sum[:].unsqueeze(3).to_broadcast([128, NT, GH, D]),
                            ALU.mult).then_inc(ctx_done, 1)

                    if first:
                        normal_stats()
                        dve.wait_ge(rstd_done, 1)
                        for t in range(NT):
                            last = nc.vector.tensor_scalar(xn[:, t], xin[:, p, t], ln_mv[:, p, t, 0:1],
                                                           ln_rstd[:, p, t:t + 1], ALU.subtract, ALU.mult)
                        last.then_inc(xn_done, 1)
                        dve.wait_ge(weights_in, 32)
                        nc.vector.tensor_copy(ident_bf[:], ident[:]).then_inc(ident_done, 1)
                        nc.vector.memset(v_ext[0][:], 0.0)
                        nc.vector.memset(v_ext[1][:], 0.0).then_inc(v_zeroed, 1)
                        dve.wait_ge(v_zeroed, 1)
                        for v in v_ext:
                            last = nc.vector.memset(v[:, :, :, D:D + 1], 1.0)
                        last.then_inc(v_preset, 1)

                    def split_max(ahead, half):
                        dve.wait_ge(max_taken, st.count(TILES, ahead, TILES // 2 * (half + 1)))
                        dve.wait_ge(maxT_ready, st.count(2, ahead - 1, half + 1))
                        nc.vector.tensor_copy(max_split[:, half, :, 0], neg_max[:, half]).then_inc(max_hi_done, 1)
                        dve.wait_ge(max_hi_done, st.count(2, ahead, half + 1))
                        nc.vector.tensor_tensor(max_rest[:], neg_max[:, half], max_split[:, half, :, 0],
                                                ALU.subtract).then_inc(max_rest_done, 1)
                        dve.wait_ge(max_rest_done, st.count(2, ahead, half + 1))
                        nc.vector.tensor_copy(max_split[:, half, :, 1], max_rest[:]).then_inc(max_mid_done, 1)
                        dve.wait_ge(max_mid_done, st.count(2, ahead, half + 1))
                        nc.vector.tensor_tensor(max_split[:, half, :, 2], max_rest[:], max_split[:, half, :, 1],
                                                ALU.subtract).then_inc(max_split_done, 1)

                    def between(u):
                        if u == AT_STATS and st.has(2) and not first:
                            normal_stats()
                        if st.has(2) and u == AT_Q:
                            rest(q_split, q_rest, q_hi_done, q_rest_done, q_mid_done, q_lo_done)
                        if st.has(2) and u == AT_K:
                            rest(k_split, k_rest, k_hi_done, k_rest_done, k_mid_done, k_lo_done)
                            if first:
                                nc.vector.memset(q_rows[1][:], 0.0).then_inc(q_rows_preset, 1)
                        if u == AT_CTX and st.has(-1):
                            normal_ctx(-1, NG - 1)
                        if u % NT == AT_CTX and u > AT_CTX and st.has(0):
                            normal_ctx(0, u // NT - 1)

                    tile = 0
                    for u in range(UNITS):
                        if u == AT_MAX[1] - 1 and st.has(0):
                            split_max(0, 1)
                        if u == AT_MAX[0] - 2 and st.has(1):
                            split_max(1, 0)
                        for n in range(GH + 1):
                            if n == 2:
                                between(u)
                            if n < MAX_TILES[u] and st.has(1):
                                dve.wait_ge(max_scored, st.count(TILES, 1, tile + 1))
                                h, t = divmod(tile, NT)
                                half, k = divmod(h, HALF)
                                if tile % (TILES // 2) == 0:
                                    dve.wait_ge(max_split_done, st.count(2, 0, half + 1))
                                nc.vector.reduce_max(neg_max[:, half, t, k:k + 1], max_ps[:, tile % BANKS], AX.X,
                                                     negate=True).then_inc(max_taken, 1)
                                tile += 1

            @block.scalar
            def _(act):
                for st in steps(act):
                    p, o = st.slot, (st.slot + 1) % 2

                    def take_context(ahead, g):
                        act.wait_ge(pv_done, st.count(UNITS, ahead, NT * (g + 1)))
                        act.wait_ge(ctx_ready, st.count(NG, ahead, g))
                        nc.scalar.copy(ctxT[:], pv_ps[:]).then_inc(ctxT_done, 1)

                    def take_max(ahead, half):
                        act.wait_ge(maxT_ready, st.count(2, ahead, half + 1))
                        act.wait_ge(max_written, st.count(32, ahead - 1, 16 * (half + 1)))
                        nc.scalar.copy(maxT[:, half], maxT_ps).then_inc(maxT_done, 1)

                    for u in range(UNITS):
                        if u == 1 and st.has(-1):
                            take_context(-1, NG - 1)
                        if u % NT == 1 and u > 1 and st.has(0):
                            take_context(0, u // NT - 1)
                        if u == AT_XT and st.has(2):
                            act.wait_ge(xT_ready, st.count(1, 2, 1))
                            act.wait_ge(v_ready, st.count(1, 0, 1))
                            nc.scalar.copy(xnT[:, p], misc_ps[:]).then_inc(xnT_done, 1)
                        if u == AT_Q and st.has(2):
                            act.wait_ge(q_ready, st.count(1, 2, 1))
                            act.wait_ge(q_written, st.count(48, 1, 48))
                            nc.scalar.copy(q_split[:, 0], misc_ps[:]).then_inc(q_hi_done, 1)
                        if u == AT_K and st.has(2):
                            act.wait_ge(k_ready, st.count(1, 2, 1))
                            act.wait_ge(k_written, st.count(48, 1, 48))
                            nc.scalar.copy(k_split[:, 0], misc_ps[:]).then_inc(k_hi_done, 1)
                        if u == AT_V and st.has(1):
                            act.wait_ge(v_ready, st.count(1, 1, 1))
                            act.wait_ge(v_preset, 1)
                            act.wait_ge(pv_done, st.count(UNITS, -1, UNITS))
                            nc.scalar.copy(v_ext[o][:, :, :, 0:D],
                                           misc_ps[:].rearrange("p (t h d) -> p t h d", t=NT, d=D)).then_inc(v_done, 1)
                        if u == AT_MAX[0] and st.has(1):
                            take_max(1, 0)
                        if u == AT_MAX[1] and st.has(0):
                            take_max(0, 1)
                        if st.has(0):
                            for j in range(GH):
                                act.wait_ge(scored, st.count(TILES, 0, GH * u + j + 1))
                                act.wait_ge(pv_done, st.count(UNITS, 0, u - 1))
                                nc.scalar.activation(probs[:, u % 2, j], score_ps[:, (GH * u + j) % BANKS], ACT.Exp,
                                                     scale=SCALE).then_inc(probs_done, 1)

            @block.tensor
            def _(pe):
                pe.wait_ge(weights_in, 32)
                pe.wait_ge(ident_done, 1)
                for st in steps(pe):
                    p, o = st.slot, (st.slot + 1) % 2

                    def score_for_max(tile):
                        h, t = divmod(tile, NT)
                        if tile % (TILES // 2) == 0:
                            pe.wait_ge(rows_in[tile // (TILES // 2)], st.count(192, 1, 192))
                        pe.wait_ge(max_taken, st.count(TILES, 1, bank_free(tile)))
                        nc.tensor.matmul(max_ps[:, tile % BANKS], q_rows[o][0:MAX_ROW, h, t * 128:(t + 1) * 128],
                                         k_rows[o][0:MAX_ROW, h, :], start=True, stop=True).then_inc(max_scored, 1)

                    def score(u, j):
                        g, t = divmod(u, NT)
                        h = GH * g + j
                        if u % (UNITS // 2) == 0 and j == 0:
                            pe.wait_ge(max_rows_in, st.count(32, 0, 16 * (u // (UNITS // 2) + 1)))
                        pe.wait_ge(probs_done, st.count(TILES, 0, bank_free(GH * u + j)))
                        nc.tensor.matmul(score_ps[:, (GH * u + j) % BANKS], k_rows[p][:, h, t * 128:(t + 1) * 128],
                                         q_rows[p][:, h, :], start=True, stop=True).then_inc(scored, 1)

                    def weigh(ahead, u):
                        g, t = divmod(u, NT)
                        pe.wait_ge(probs_done, st.count(TILES, ahead, GH * (u + 1)))
                        if u == 0:
                            pe.wait_ge(v_done, st.count(1, ahead, 1))
                        if t == 0:
                            pe.wait_ge(ctxT_done, st.count(NG, ahead, g))
                        for j in range(GH):
                            last = nc.tensor.matmul(pv_ps[32 * j:32 * j + 32, :], v_ext[(p + ahead) % 2][:, t, GH * g + j],
                                                    probs[:, u % 2, j], start=t == 0, stop=t == NT - 1)
                        last.then_inc(pv_done, 1)

                    def transpose_context(ahead, g):
                        pe.wait_ge(ctxT_done, st.count(NG, ahead, g + 1))
                        for t in range(NT):
                            last = nc.tensor.transpose(misc_ps[:, t * 128:(t + 1) * 128],
                                                       ctxT[:, t * 128:(t + 1) * 128], ident[:])
                        last.then_inc(ctx_ready, 1)

                    def transpose_max(ahead, half):
                        pe.wait_ge(max_split_done, st.count(2, ahead, half + 1))
                        pe.sem_inc(stood, 1)
                        for t in range(NT):
                            last = nc.tensor.transpose(maxT_ps[:, t * 128:(t + 1) * 128],
                                                       max_split[:, half, t].rearrange("p j h -> p (j h)"), ident_bf[:])
                        last.then_inc(maxT_ready, 1)

                    tile = 0
                    for u in range(UNITS):
                        if u == AT_CTX and st.has(-1):
                            pe.wait_ge(ctx_done, st.count(NG, -1, NG - 1))
                            if st.has(0):
                                pe.wait_ge(maxT_done, st.count(2, 0, 2))
                            transpose_context(-1, NG - 1)
                        if u % NT == AT_CTX and u > AT_CTX and st.has(0):
                            if u == AT_CTX + NT and st.has(2):
                                pe.wait_ge(q_rest_done, st.count(1, 2, 1))
                            if u == AT_CTX + 2 * NT and st.has(1):
                                pe.wait_ge(v_done, st.count(1, 1, 1))
                            if u == AT_CTX + 3 * NT and st.has(1):
                                pe.wait_ge(maxT_done, st.count(2, 1, 1))
                            pe.wait_ge(ctx_done, st.count(NG, 0, u // NT - 1))
                            transpose_context(0, u // NT - 1)
                        if u == AT_XT and st.has(2):
                            pe.wait_ge(xn_done, st.count(1, 2, 1))
                            pe.wait_ge(maxT_done, st.count(2, 0, 2))
                            pe.wait_ge(ctx_done, st.count(NG, -1, NG))
                            for t in range(NT):
                                last = nc.tensor.transpose(misc_ps[:, t * 128:(t + 1) * 128], xn[:, t], ident[:])
                            last.then_inc(xT_ready, 1)
                        if u == AT_Q and st.has(2):
                            pe.wait_ge(xnT_done, st.count(1, 2, 1))
                            nc.tensor.matmul(misc_ps[:], w_sb[:, 0:H], xnT[:, p], start=True, stop=True).then_inc(q_ready, 1)
                        if u == AT_K and st.has(2):
                            pe.wait_ge(q_rest_done, st.count(1, 2, 1))
                            pe.wait_ge(ctx_done, st.count(NG, 0, 1))
                            nc.tensor.matmul(misc_ps[:], w_sb[:, H:2 * H], xnT[:, p], start=True, stop=True).then_inc(k_ready, 1)
                        if u == AT_V and st.has(1):
                            if st.has(2):
                                pe.wait_ge(k_rest_done, st.count(1, 2, 1))
                            if st.has(0):
                                pe.wait_ge(ctx_done, st.count(NG, 0, 1))
                            for t in range(NT):
                                last = nc.tensor.matmul(misc_ps[:, t * H:(t + 1) * H], xnT[:, o, t * 128:(t + 1) * 128],
                                                        w_sb[:, 2 * H:3 * H], start=True, stop=True)
                            last.then_inc(v_ready, 1)
                        if u == AT_MAX[0] and st.has(1):
                            pe.wait_ge(v_done, st.count(1, 1, 1))
                            if st.has(0):
                                pe.wait_ge(ctx_done, st.count(NG, 0, NG - 2))
                            transpose_max(1, 0)
                        if u == AT_MAX[1] and st.has(0):
                            if st.has(-1):
                                pe.wait_ge(ctx_done, st.count(NG, -1, NG - 1))
                            if st.has(1):
                                pe.wait_ge(v_done, st.count(1, 0, 1))
                            transpose_max(0, 1)

                        for n in range(GH + 1):
                            if n < GH and st.has(0):
                                score(u, n)
                            if n == GH and u == 0 and st.has(-1):
                                weigh(-1, UNITS - 1)
                            if n == GH and u > 0 and st.has(0):
                                weigh(0, u - 1)
                            if n < MAX_TILES[u] and st.has(1):
                                score_for_max(tile)
                                tile += 1

        with ExitStack() as two:
            RING = 3
            ln_stats = sb("ln_stats2", [128, NT, nc.vector.BN_STATS_DIM], FP32, two)
            ln_mv = sb("ln_mv2", [128, NT, 2], FP32, two)
            ln_rstd = sb("ln_rstd2", [128, NT], FP32, two)
            xn = sb("xn2", [128, NT, H], FP32, two)
            xnT_hi = sb("xnT2_hi", [128, RING, S], FP32R, two)
            xnT_lo = sb("xnT2_lo", [128, RING, S], FP32R, two)
            top = sb("top", [128, NT], FP32, two)
            prob = sb("prob", [128, NT, E], FP32, two)
            norm = sb("norm", [128, NT], FP32, two)
            beats = sb("beats", [128, NT, E, E], FP32, two)
            ties = sb("ties", [128, NT, E, E], FP32, two)
            rank = sb("rank", [128, NT, E], FP32, two)
            route = sb("route", [128, E, NT], FP32, two)
            routeT = sb("routeT", [E * NT, 128], FP32, two)
            route_all = sb("route_all", [128, RING, E, S], FP32, two)
            gate_act = sb("gate_act", [128, 2, S], FP32, two)
            gate_wgt = sb("gate_wgt", [128, 2, S], FP32, two)
            hidden = sb("hidden", [128, 3, S], FP32, two)
            yT = sb("yT", [128, S], FP32, two)
            out_sb = sb("out_sb", [128, RING, NT, H], FP32, two)

            gate_ps = ps("gate_ps", [128, 2, S], FP32, two)
            up_ps = ps("up_ps", [128, 2, S], FP32, two)
            y_ps = ps("y_ps", [128, S], FP32, two)
            xT_ps = ps("xT_ps", [128, S], FP32, two)
            route_ps = ps("route_ps", [128, 512], FP32, two)
            yt_ps = ps("yt_ps", [128, S], FP32, two)
            logits = route_ps[:, 0:NT * E].rearrange("p (t e) -> p t e", t=NT)
            routeT_ps = route_ps[0:E * NT, 128:256]

            dve_link = sem("dve_link", two)
            stats_done = sem("stats2_done", two)
            mv_done = sem("mv2_done", two)
            var_done = sem("var2_done", two)
            rstd_done = sem("rstd2_done", two)
            xn_done = sem("xn2_done", two)
            xT_ready = sem("xT2_ready", two)
            xnT_hi_done = sem("xnT2_hi_done", two)
            xnT_lo_done = sem("xnT2_lo_done", two)
            logits_ready = sem("logits_ready", two)
            logits_shifted = sem("logits_shifted", two)
            exp_done = sem("exp_done", two)
            route_done = sem("route_done", two)
            routeT_ready = sem("routeT_ready", two)
            routeT_done = sem("routeT_done", two)
            route_written = sem("route_written", two)
            route_in = [sem(f"route_in{i}", two) for i in range(RING)]
            gate_ready = sem("gate_ready", two)
            up_ready = sem("up_ready", two)
            gate_act_done = sem("gate_act_done", two)
            gate_wgt_done = sem("gate_wgt_done", two)
            hidden_done = sem("hidden_done", two)
            down_done = sem("down_done", two)
            yT_done = sem("yT_done", two)
            yt_ready = sem("yt_ready", two)
            out_done = sem("out_done", two)
            stored = [sem(f"stored{i}", two) for i in range(RING)]

            LAG = 2
            AT_CENTRE, AT_XT2, AT_LOGITS, AT_ROUTE, AT_Y, AT_YT = 2, 4, 5, 3, 2, 3
            AT_WEIGHTS = 1
            LINKS_BEFORE = 9
            LINKS = 16

            block = two.enter_context(nc.Block())

            def steps2(engine):
                return walk(engine, (-2, -1, 0), RING, (B - 4) // RING, range(B - 3, B + 1), B)

            def hidden_slot(st, ahead, e):
                return (((st.slot + ahead) % RING) * E + e) % 3


            @block.sync
            def _(sp):
                for i in range(RING):
                    sp.sem_inc(stored[i], 16)
                for st in steps2(sp):
                    p = st.slot
                    if st.has(-1):
                        o = (p + RING - 1) % RING
                        sp.wait_ge(out_done, st.count(1, -1, 2))
                        sp.sem_inc(stood, 1)
                        sp.dma_start(out_v[bass.ds(st.number - 1, 1)].rearrange("o p t h -> (o p) t h"),
                                     out_sb[:, o]).then_inc(stored[o], 16)
                    if st.has(1):
                        o = (p + 1) % RING
                        sp.wait_ge(routeT_done, st.count(1, 1, 1))
                        sp.dma_start(route_scratch[o].rearrange("e t p -> (e t) p"), routeT[:]).then_inc(route_written, 16)
                        sp.wait_ge(route_written, st.count(16, 1, 16))
                        sp.sem_inc(stood, 1)
                        sp.wait_ge(gate_wgt_done, st.count(E, -1, 1))
                        sp.dma_start(route_all[:, o].rearrange("p e s -> p (e s)"),
                                     route_scratch[o].rearrange("e t p -> (e t p)").partition_broadcast(128)
                                     ).then_inc(route_in[o], 16)
                for i in range(RING):
                    sp.wait_ge(stored[i], 16 + 16 * len(range(i, B, RING)))

            @block.gpsimd
            def _(pool):
                for st in steps2(pool):
                    p = st.slot
                    for e in range(E):
                        if st.has(0):
                            n = e % 2
                            if e == 0:
                                pool.wait_ge(route_in[st.buffer(0)], st.loads(0))
                            pool.wait_ge(gate_act_done, st.count(E, 0, e + 1))
                            pool.sem_inc(stood, 1)
                            pool.wait_ge(hidden_done, st.count(E, 0, e - 1))
                            pool.sem_inc(stood, 1)
                            nc.gpsimd.tensor_tensor(gate_wgt[:, n], gate_act[:, n], route_all[:, p, e],
                                                    ALU.mult).then_inc(gate_wgt_done, 1)
                        if e == 0 and st.has(2):
                            pool.wait_ge(mv_done, st.count(1, 2, 1))
                            pool.sem_inc(stood, 1)
                            pool.wait_ge(xn_done, st.count(1, 1, 1))
                            pool.sem_inc(stood, 1)
                            nc.gpsimd.tensor_scalar(ln_var[:], ln_mv[:, :, 1], LN_EPS, None, ALU.add).then_inc(var_done, 1)
                            pool.wait_ge(var_done, st.count(1, 2, 1))
                            pool.sem_inc(stood, 1)
                            nc.gpsimd.tensor_tensor(ln_rstd[:], ln_var[:], minus_half[:], ALU.pow).then_inc(rstd_done, 1)

            @block.vector
            def _(dve):
                dve.sem_inc(out_done, 1)
                for st in steps2(dve):
                    p = st.slot
                    front = (p + 2) % RING
                    links = {2: 0, 1: LINKS_BEFORE}

                    def link(instruction, ahead=2):
                        instruction.then_inc(dve_link, 1)
                        links[ahead] += 1
                        dve.wait_ge(dve_link, st.count(LINKS, ahead, links[ahead]))

                    def normalise():
                        at = (st.number + 2) * S
                        tiles = [x_all[:, bass.ds(at + t * H, H)] for t in range(NT)]
                        for t in range(NT):
                            last = nc.vector.bn_stats(ln_stats[:, t], tiles[t])
                        last.then_inc(stats_done, 1)
                        dve.wait_ge(stats_done, st.count(1, 2, 1))
                        dve.sem_inc(stood, 1)
                        for t in range(NT - 1):
                            nc.vector.bn_aggr(ln_mv[:, t], ln_stats[:, t])
                        nc.vector.bn_aggr(ln_mv[:, NT - 1], ln_stats[:, NT - 1]).then_inc(mv_done, 1)

                    def centre():
                        at = (st.number + 2) * S
                        tiles = [x_all[:, bass.ds(at + t * H, H)] for t in range(NT)]
                        dve.wait_ge(rstd_done, st.count(1, 2, 1))
                        dve.wait_ge(xT_ready, st.count(1, 1, 1))
                        for t in range(NT):
                            last = nc.vector.tensor_scalar(xn[:, t], tiles[t], ln_mv[:, t, 0:1], ln_rstd[:, t:t + 1],
                                                           ALU.subtract, ALU.mult)
                        last.then_inc(xn_done, 1)

                    def spread(v):
                        return v[:].unsqueeze(2).to_broadcast([128, NT, E])

                    def softmax_shift():
                        dve.wait_ge(logits_ready, st.count(1, 2, 1))
                        link(nc.vector.reduce_max(top[:], logits, AX.X))
                        nc.vector.tensor_tensor(prob[:], logits, spread(top), ALU.subtract).then_inc(logits_shifted, 1)

                    def softmax_divide():
                        dve.wait_ge(exp_done, st.count(1, 2, 1))
                        link(nc.vector.reduce_sum(norm[:], prob[:], AX.X))
                        link(nc.vector.reciprocal(norm[:], norm[:]))
                        link(nc.vector.tensor_tensor(prob[:], prob[:], spread(norm), ALU.mult))

                    def compare():
                        mine = prob[:].unsqueeze(3).to_broadcast([128, NT, E, E])
                        other = prob[:].unsqueeze(2).to_broadcast([128, NT, E, E])
                        nc.vector.tensor_tensor(beats[:], other, mine, ALU.is_gt)
                        link(nc.vector.tensor_tensor(ties[:], other, mine, ALU.is_equal))
                        link(nc.vector.tensor_tensor(ties[:], ties[:], earlier[:], ALU.mult))

                    def keep_two():
                        link(nc.vector.tensor_tensor(beats[:], beats[:], ties[:], ALU.add))
                        link(nc.vector.reduce_sum(rank[:], beats[:], AX.X))
                        link(nc.vector.scalar_tensor_tensor(out=prob[:], in0=rank[:], scalar=1.5, in1=prob[:],
                                                            op0=ALU.is_lt, op1=ALU.mult))

                    def normalise_weights():
                        link(nc.vector.reduce_sum(norm[:], prob[:], AX.X), 1)
                        link(nc.vector.tensor_scalar(norm[:], norm[:], TOP_EPS, None, ALU.add), 1)
                        link(nc.vector.reciprocal(norm[:], norm[:]), 1)
                        link(nc.vector.tensor_tensor(prob[:], prob[:], spread(norm), ALU.mult), 1)
                        link(nc.vector.reduce_sum(norm[:], prob[:], AX.X), 1)
                        link(nc.vector.tensor_scalar(norm[:], norm[:], TOP_EPS, None, ALU.add), 1)
                        link(nc.vector.reciprocal(norm[:], norm[:]), 1)
                        assert links[1] == LINKS
                        dve.wait_ge(routeT_ready, st.count(1, 0, 1))
                        nc.vector.tensor_tensor(route[:].rearrange("p e t -> p t e"), prob[:], spread(norm),
                                                ALU.mult).then_inc(route_done, 1)

                    def hide(ahead, e):
                        dve.wait_ge(gate_wgt_done, st.count(E, ahead, e + 1))
                        dve.wait_ge(up_ready, st.count(E, ahead, e + 1))
                        dve.wait_ge(down_done, st.count(E, ahead, e - 2))
                        nc.vector.tensor_tensor(hidden[:, hidden_slot(st, ahead, e)], up_ps[:, e % 2], gate_wgt[:, e % 2],
                                                ALU.mult).then_inc(hidden_done, 1)

                    for e in range(E):
                        if e == 0 and st.has(-1):
                            hide(-1, E - 1)
                        if e > 0 and st.has(0):
                            hide(0, e - 1)
                        if e == 0 and st.has(2):
                            normalise()
                        if e == AT_WEIGHTS and st.has(1):
                            normalise_weights()
                        if st.has(2):
                            if e == AT_CENTRE:
                                centre()
                            if e == AT_XT2:
                                dve.wait_ge(xnT_hi_done, st.count(1, 2, 1))
                                nc.vector.tensor_tensor(xnT_lo[:, front], xT_ps[:], xnT_hi[:, front].bitcast(FP32),
                                                        ALU.subtract).then_inc(xnT_lo_done, 1)
                            if e == AT_LOGITS:
                                softmax_shift()
                            if e == AT_LOGITS + 1:
                                softmax_divide()
                                compare()
                            if e == AT_LOGITS + 2:
                                keep_two()
                                assert links[2] == LINKS_BEFORE
                        if e == AT_YT and st.has(-1):
                            o = (p + RING - 1) % RING
                            dve.wait_ge(yt_ready, st.count(1, -1, 2))
                            dve.wait_ge(stored[st.buffer(-1)], st.loads(-1))
                            nc.vector.tensor_tensor(out_sb[:, o].rearrange("p t h -> p (t h)"), yt_ps[:],
                                                    x_all[:, bass.ds((st.number - 1) * S, S)], ALU.add).then_inc(out_done, 1)

            @block.scalar
            def _(act):
                for st in steps2(act):
                    p = st.slot
                    front = (p + 2) % RING
                    for e in range(E):
                        if e == AT_Y and st.has(-1):
                            act.wait_ge(down_done, st.count(E, -1, E))
                            act.wait_ge(yt_ready, st.count(1, -2, 2))
                            nc.scalar.copy(yT[:], y_ps[:]).then_inc(yT_done, 1)
                        if e == AT_XT2 and st.has(2):
                            act.wait_ge(xT_ready, st.count(1, 2, 1))
                            act.wait_ge(up_ready, st.count(E, -1, E))
                            nc.scalar.copy(xnT_hi[:, front], xT_ps[:]).then_inc(xnT_hi_done, 1)
                        if e == AT_ROUTE and st.has(1):
                            act.wait_ge(routeT_ready, st.count(1, 1, 1))
                            act.wait_ge(route_written, st.count(16, 0, 16))
                            nc.scalar.copy(routeT[:], routeT_ps).then_inc(routeT_done, 1)
                        if st.has(0):
                            act.wait_ge(gate_ready, st.count(E, 0, e + 1))
                            act.wait_ge(gate_wgt_done, st.count(E, 0, e - 1))
                            nc.scalar.activation(gate_act[:, e % 2], gate_ps[:, e % 2], ACT.Silu).then_inc(gate_act_done, 1)
                        if e == AT_LOGITS and st.has(2):
                            act.wait_ge(logits_shifted, st.count(1, 2, 1))
                            nc.scalar.activation(prob[:], prob[:], ACT.Exp).then_inc(exp_done, 1)

            @block.tensor
            def _(pe):
                pe.sem_inc(yt_ready, 1)
                for st in steps2(pe):
                    p = st.slot
                    front = (p + 2) % RING

                    def project(where, e, columns):
                        nc.tensor.matmul(where, w_gu_hi[:, e, columns], xnT_hi[:, p], start=True, stop=False)
                        nc.tensor.matmul(where, w_gu_hi[:, e, columns], xnT_lo[:, p], start=False, stop=False)
                        return nc.tensor.matmul(where, w_gu_lo[:, e, columns], xnT_hi[:, p], start=False, stop=True)

                    def down(ahead, e):
                        pe.wait_ge(hidden_done, st.count(E, ahead, e + 1))
                        if e == 0:
                            pe.wait_ge(yT_done, st.count(1, ahead - 1, 1))
                        nc.tensor.matmul(y_ps[:], w_down[:, e], hidden[:, hidden_slot(st, ahead, e)], start=e == 0,
                                         stop=e == E - 1).then_inc(down_done, 1)

                    for e in range(E):
                        if e == AT_XT2 and st.has(2):
                            pe.wait_ge(xn_done, st.count(1, 2, 1))
                            pe.wait_ge(xnT_lo_done, st.count(1, 1, 1))
                            for t in range(NT):
                                last = nc.tensor.transpose(xT_ps[:, t * 128:(t + 1) * 128], xn[:, t], ident[:])
                            last.then_inc(xT_ready, 1)
                        if e == AT_LOGITS and st.has(2):
                            pe.wait_ge(xnT_lo_done, st.count(1, 2, 1))
                            pe.wait_ge(routeT_done, st.count(1, 1, 1))
                            for t in range(NT):
                                tokens = slice(t * 128, (t + 1) * 128)
                                where = route_ps[:, t * E:(t + 1) * E]
                                nc.tensor.matmul(where, xnT_hi[:, front, tokens], w_gate_hi[:], start=True, stop=False)
                                nc.tensor.matmul(where, xnT_hi[:, front, tokens], w_gate_lo[:], start=False, stop=False)
                                last = nc.tensor.matmul(where, xnT_lo[:, front, tokens], w_gate_hi[:],
                                                        start=False, stop=True)
                            last.then_inc(logits_ready, 1)
                        if e == AT_ROUTE and st.has(1):
                            pe.wait_ge(route_done, st.count(1, 1, 1))
                            nc.tensor.transpose(routeT_ps, route[:].rearrange("p e t -> p (e t)"), ident[:]).then_inc(routeT_ready, 1)
                        if e == AT_YT and st.has(-1):
                            pe.wait_ge(yT_done, st.count(1, -1, 1))
                            pe.wait_ge(out_done, st.count(1, -2, 2))
                            for t in range(NT):
                                last = nc.tensor.transpose(yt_ps[:, t * 128:(t + 1) * 128], yT[:, t * 128:(t + 1) * 128], ident[:])
                            last.then_inc(yt_ready, 1)
                        if st.has(0):
                            pe.wait_ge(gate_act_done, st.count(E, 0, e - 1))
                            project(gate_ps[:, e % 2], e, slice(0, H)).then_inc(gate_ready, 1)
                            pe.wait_ge(hidden_done, st.count(E, 0, e - 1))
                            project(up_ps[:, e % 2], e, slice(H, 2 * H)).then_inc(up_ready, 1)
                        if e < LAG and st.has(-1):
                            down(-1, E - LAG + e)
                        if e >= LAG and st.has(0):
                            down(0, e - LAG)


_INS = ['L0_attn_embeddings', 'L0_attn_w_qkv', 'L0_ffn_gate_w', 'L0_ffn_gate_up_proj', 'L0_ffn_down_proj']
_OUTS = [((16, 512, 128), 'float32')]


def kernel(**inputs):
    import numpy as _np
    import concourse.bacc as _bacc
    from concourse import mybir as _mybir
    from concourse.bass_utils import run_bass_kernel_spmd as _run

    nc = _bacc.Bacc("TRN2", target_bir_lowering=False, num_devices=1)
    arrays, args = {}, []
    for name in _INS + ['identity']:
        a = _np.eye(128, dtype=_np.float32) if name == 'identity' else _np.asarray(inputs[name])
        if name == 'L0_ffn_gate_w':
            a = a.T
        a = _np.ascontiguousarray(a)
        arrays[f"in_{name}_dram"] = a
        args.append(nc.dram_tensor(f"in_{name}_dram", a.shape, _mybir.dt.from_np(a.dtype), kind="ExternalInput").ap())
    for i, (shape, dtype) in enumerate(_OUTS):
        dt = _mybir.dt.from_np(_np.dtype(dtype))
        args.append(nc.dram_tensor(f"out_{i}_dram", shape, dt, kind="ExternalOutput").ap())
    attention_moe_kernel(nc, *args)
    r = _run(nc, [arrays], core_ids=[0])
    got = tuple(r.results[0][f"out_{i}_dram"] for i in range(len(_OUTS)))
    return got[0]
```
